# Optimizing a Trainium2 kernel written in Bass

```python
import numpy as np
import jax
import jax.numpy as jnp

def _softmax(x, axis=-1):
    return jax.nn.softmax(x, axis=axis)

def _gelu(x):
    return jax.nn.gelu(x, approximate=True)

def _silu(x):
    return jax.nn.silu(x)

def _sigmoid(x):
    return jax.nn.sigmoid(x)

def _layernorm(x, axis=-1, eps=1e-05):
    m = jnp.mean(x, axis=axis, keepdims=True)
    v = jnp.var(x, axis=axis, keepdims=True)
    return (x - m) / jnp.sqrt(v + eps)

def _scatter_add(tgt, idx, src, axis=0):
    return tgt.at[idx].add(src)

def _segment_sum(src, seg, n):
    return jax.ops.segment_sum(src, seg, n)
kernel_name = 'mk_decoder_postln_d1_seqx_r4_c3e902'

def setup_inputs(seed: int=0):
    np.random.seed(seed)
    _w = jnp.asarray

    def _rec_inputs():
        import jax
        import jax.numpy as jnp
        _rk = jax.random.key(seed)
        x = 0.000341 + 1 * jax.random.normal(jax.random.fold_in(_rk, 1), (8, 256, 512), jnp.float32)
        _lenS = 256 - jax.random.randint(jax.random.fold_in(_rk, 7), (8,), 0, max(1, 256 // 4) + 1, jnp.int32)
        _lenS2 = 256 - jax.random.randint(jax.random.fold_in(_rk, 8), (8,), 0, max(1, 256 // 4) + 1, jnp.int32)
        _ctx_2048P = jax.random.normal(jax.random.fold_in(_rk, 11), (8, 16, 512), jnp.float32)
        _ctx_2048c = jax.random.dirichlet(jax.random.fold_in(_rk, 511), 0.3 * jnp.ones((16,), jnp.float32), (8, 256))
        _ctx_2048t = jnp.einsum('bsk,bkd->bsd', _ctx_2048c, _ctx_2048P)
        _ctx_2048t = _ctx_2048t * jax.lax.rsqrt(jnp.mean(jnp.square(_ctx_2048t)) + 1e-12) * 0.953939
        ctx_2048 = -1.47943e-05 + 1.00017 * (_ctx_2048t + 0.3 * jax.random.normal(jax.random.fold_in(_rk, 611), (8, 256, 512), jnp.float32))
        return (x, ctx_2048)
    x, ctx_2048 = _rec_inputs()

    def _L0_attn_setup():
        import jax, jax.numpy as jnp
        import numpy as np
        BLOCK = 64
        key = jax.random.key(seed)
        ks = jax.random.split(key, 6)
        b, n, hid = (2, 1024, 512)
        h, d = (16, 128)
        x = jax.random.normal(ks[0], (b, n, hid), dtype=jnp.float32)
        slope_rate = jax.random.uniform(ks[1], (h, 1, 1), dtype=jnp.float32)
        Wqkv = jax.random.normal(ks[2], (3 * h * d, hid), dtype=jnp.float32) * 0.02
        Wg = jax.random.normal(ks[3], (h * d, hid), dtype=jnp.float32) * 0.02
        norm_w = jnp.ones((h * d,), dtype=jnp.float32)
        Wo = jax.random.normal(ks[4], (hid, h * d), dtype=jnp.float32) * 0.02
        return {'x': x, 'slope_rate': slope_rate, 'Wqkv': Wqkv, 'Wg': Wg, 'norm_w': norm_w, 'Wo': Wo}
    _L0_attn_all = _L0_attn_setup()
    _L0_attn_in = {k: v for k, v in _L0_attn_all.items() if k in ('slope_rate', 'Wqkv', 'Wg', 'norm_w', 'Wo')}
    del _L0_attn_all

    def _L0_xattn_setup():
        import jax, jax.numpy as jnp
        import numpy as np

        def _wkv(time_decay, time_first, k, v):
            w = -jnp.exp(time_decay)
            u = time_first
            B, T, C = k.shape
            aa = jnp.zeros((B, C), dtype=k.dtype)
            bb = jnp.zeros((B, C), dtype=k.dtype)
            pp = jnp.full((B, C), -1e+38, dtype=k.dtype)

            def step(carry, kv_t):
                aa, bb, pp = carry
                kt, vt = kv_t
                ww = u + kt
                q = jnp.maximum(pp, ww)
                e1 = jnp.exp(pp - q)
                e2 = jnp.exp(ww - q)
                y_t = (e1 * aa + e2 * vt) / (e1 * bb + e2)
                ww2 = pp + w
                q2 = jnp.maximum(ww2, kt)
                e1b = jnp.exp(ww2 - q2)
                e2b = jnp.exp(kt - q2)
                new_carry = (e1b * aa + e2b * vt, e1b * bb + e2b, q2)
                return (new_carry, y_t)
            ks = jnp.transpose(k, (1, 0, 2))
            vs = jnp.transpose(v, (1, 0, 2))
            _, ys = jax.lax.scan(step, (aa, bb, pp), (ks, vs))
            return jnp.transpose(ys, (1, 0, 2))
        key = jax.random.key(seed)
        k1, k2, k3, k4 = jax.random.split(key, 4)
        B, T, C = (8, 256, 512)
        return {'batch_size': B, 'seq_len': T, 'embedding_dim': C, 'time_decay': jax.random.normal(k1, (C,), dtype=jnp.float32), 'time_first': jax.random.normal(k2, (C,), dtype=jnp.float32), 'k': jax.random.normal(k3, (B, T, C), dtype=jnp.float32), 'v': jax.random.normal(k4, (B, T, C), dtype=jnp.float32)}
    _L0_xattn_all = _L0_xattn_setup()
    _L0_xattn_in = {k: v for k, v in _L0_xattn_all.items() if k in ('time_decay', 'time_first')}
    del _L0_xattn_all

    def _L0_ffn_setup():
        import jax, jax.numpy as jnp
        import numpy as np
        EPS = 1e-06
        Q_B = 128.0

        def layer_norm(x):
            mean = jnp.mean(x, axis=-1, keepdims=True)
            var = jnp.var(x, axis=-1, keepdims=True)
            return (x - mean) / jnp.sqrt(var + EPS)

        def absmax_quant(x):
            gamma = jnp.max(jnp.abs(x), axis=-1, keepdims=True)
            x_hat = jnp.clip(x * Q_B / gamma, -Q_B + EPS, Q_B - EPS)
            return x_hat * gamma / Q_B

        def ternarize_weights(w):
            gamma = jnp.mean(jnp.abs(w))
            return jnp.sign(jnp.round(w / (gamma + EPS))) * gamma

        def bitlinear(x, w):
            xn = layer_norm(x)
            x_hat = xn + jax.lax.stop_gradient(absmax_quant(xn) - xn)
            w_hat = w + jax.lax.stop_gradient(ternarize_weights(w) - w)
            return jnp.einsum('bsd,od->bso', x_hat, w_hat)
        key = jax.random.key(seed)
        k1, k2, k3 = jax.random.split(key, 3)
        B, S, D = (4, 512, 512)
        x = jax.random.normal(k1, (B, S, D), dtype=jnp.float32)
        w_fc = jax.random.normal(k2, (4 * D, D), dtype=jnp.float32) / np.sqrt(D)
        w_proj = jax.random.normal(k3, (D, 4 * D), dtype=jnp.float32) / np.sqrt(4 * D)
        return {'x': x, 'w_fc': w_fc, 'w_proj': w_proj}
    _L0_ffn_all = _L0_ffn_setup()
    _L0_ffn_in = {k: v for k, v in _L0_ffn_all.items() if k in ('w_fc', 'w_proj')}
    del _L0_ffn_all
    return {'x': x, 'ctx_2048': ctx_2048, 'L0_attn_slope_rate': _L0_attn_in['slope_rate'], 'L0_attn_Wqkv': _L0_attn_in['Wqkv'], 'L0_attn_Wg': _L0_attn_in['Wg'], 'L0_attn_norm_w': _L0_attn_in['norm_w'], 'L0_attn_Wo': _L0_attn_in['Wo'], 'L0_xattn_time_decay': _L0_xattn_in['time_decay'], 'L0_xattn_time_first': _L0_xattn_in['time_first'], 'L0_ffn_w_fc': _L0_ffn_in['w_fc'], 'L0_ffn_w_proj': _L0_ffn_in['w_proj']}

def reference(x, ctx_2048, L0_attn_slope_rate, L0_attn_Wqkv, L0_attn_Wg, L0_attn_norm_w, L0_attn_Wo, L0_xattn_time_decay, L0_xattn_time_first, L0_ffn_w_fc, L0_ffn_w_proj):
    import jax
    import jax.numpy as jnp

    def _L0_attn_ref(x, slope_rate, Wqkv, Wg, norm_w, Wo):
        import jax, jax.numpy as jnp
        import numpy as np
        BLOCK = 64
        b, n, hid = x.shape
        h = slope_rate.shape[0]
        d = Wqkv.shape[0] // (3 * h)
        nb = n // BLOCK
        qkv = jax.nn.silu(x @ Wqkv.T).reshape(b, n, h, 3 * d)
        q, k, v = jnp.split(qkv, 3, axis=-1)
        q = q.transpose(0, 2, 1, 3)
        k = k.transpose(0, 2, 1, 3)
        v = v.transpose(0, 2, 1, 3)
        s = slope_rate.astype(jnp.float32)
        arr = jnp.arange(1, BLOCK + 1, dtype=jnp.float32)
        q_decay = jnp.exp(-s * arr[:, None])
        k_decay = jnp.exp(-s * (BLOCK - arr[:, None]))
        idx = arr[:, None] - arr[None, :]
        diag_decay = jnp.where(idx >= 0, jnp.exp(-s * idx), 0.0)
        block_decay = jnp.exp(-s * BLOCK)

        def chunk(t):
            return t.reshape(b, h, nb, BLOCK, d).transpose(2, 0, 1, 3, 4)
        qc, kc, vc = (chunk(q), chunk(k), chunk(v))

        def step(kv, qkv_blk):
            qi, ki, vi = qkv_blk
            out_nd = jnp.einsum('bhmd,bhde->bhme', qi * q_decay, kv)
            qk = jnp.einsum('bhmd,bhnd->bhmn', qi, ki) * diag_decay
            out_d = jnp.einsum('bhmn,bhne->bhme', qk, vi)
            kv_new = block_decay * kv + jnp.einsum('bhmd,bhme->bhde', ki * k_decay, vi)
            return (kv_new, out_nd + out_d)
        kv0 = jnp.zeros((b, h, d, d), dtype=jnp.float32)
        _, out_blocks = jax.lax.scan(step, kv0, (qc, kc, vc))
        out = out_blocks.transpose(1, 2, 0, 3, 4).reshape(b, h, n, d)
        out = out.transpose(0, 2, 1, 3).reshape(b, n, h * d)
        eps = jnp.finfo(jnp.float32).eps
        rms = jax.lax.rsqrt(jnp.mean(out * out, axis=-1, keepdims=True) + eps)
        out = out * rms * norm_w
        gate = jax.nn.sigmoid(x @ Wg.T)
        return gate * out @ Wo.T

    def _L0_xattn_ref(batch_size, seq_len, embedding_dim, time_decay, time_first, k, v):
        import jax, jax.numpy as jnp
        import numpy as np

        def _wkv(time_decay, time_first, k, v):
            w = -jnp.exp(time_decay)
            u = time_first
            B, T, C = k.shape
            aa = jnp.zeros((B, C), dtype=k.dtype)
            bb = jnp.zeros((B, C), dtype=k.dtype)
            pp = jnp.full((B, C), -1e+38, dtype=k.dtype)

            def step(carry, kv_t):
                aa, bb, pp = carry
                kt, vt = kv_t
                ww = u + kt
                q = jnp.maximum(pp, ww)
                e1 = jnp.exp(pp - q)
                e2 = jnp.exp(ww - q)
                y_t = (e1 * aa + e2 * vt) / (e1 * bb + e2)
                ww2 = pp + w
                q2 = jnp.maximum(ww2, kt)
                e1b = jnp.exp(ww2 - q2)
                e2b = jnp.exp(kt - q2)
                new_carry = (e1b * aa + e2b * vt, e1b * bb + e2b, q2)
                return (new_carry, y_t)
            ks = jnp.transpose(k, (1, 0, 2))
            vs = jnp.transpose(v, (1, 0, 2))
            _, ys = jax.lax.scan(step, (aa, bb, pp), (ks, vs))
            return jnp.transpose(ys, (1, 0, 2))
        assert seq_len <= 256
        return _wkv(time_decay, time_first, k, v)

    def _L0_ffn_ref(x, w_fc, w_proj):
        import jax, jax.numpy as jnp
        import numpy as np
        EPS = 1e-06
        Q_B = 128.0

        def layer_norm(x):
            mean = jnp.mean(x, axis=-1, keepdims=True)
            var = jnp.var(x, axis=-1, keepdims=True)
            return (x - mean) / jnp.sqrt(var + EPS)

        def absmax_quant(x):
            gamma = jnp.max(jnp.abs(x), axis=-1, keepdims=True)
            x_hat = jnp.clip(x * Q_B / gamma, -Q_B + EPS, Q_B - EPS)
            return x_hat * gamma / Q_B

        def ternarize_weights(w):
            gamma = jnp.mean(jnp.abs(w))
            return jnp.sign(jnp.round(w / (gamma + EPS))) * gamma

        def bitlinear(x, w):
            xn = layer_norm(x)
            x_hat = xn + jax.lax.stop_gradient(absmax_quant(xn) - xn)
            w_hat = w + jax.lax.stop_gradient(ternarize_weights(w) - w)
            return jnp.einsum('bsd,od->bso', x_hat, w_hat)
        h = bitlinear(x, w_fc)
        h = jax.nn.gelu(h, approximate=False)
        return bitlinear(h, w_proj)
    x = _layernorm(x + _L0_attn_ref(x, L0_attn_slope_rate, L0_attn_Wqkv, L0_attn_Wg, L0_attn_norm_w, L0_attn_Wo), axis=-1)
    x = _layernorm(x + _L0_xattn_ref(8, 256, 512, L0_xattn_time_decay, L0_xattn_time_first, x, ctx_2048), axis=-1)
    x = _layernorm(x + _L0_ffn_ref(x, L0_ffn_w_fc, L0_ffn_w_proj), axis=-1)
    return x

_drawn_inputs = setup_inputs


def setup_inputs(seed=0):
    import zlib

    import numpy as np

    out = dict(_drawn_inputs(seed))
    spreads = {'L0_attn_norm_w': (1.0, 0.2)}
    factors = {}
    for name, (base, spread) in spreads.items():
        noise = np.random.default_rng([zlib.crc32(name.encode()), seed]).standard_normal(out[name].shape)
        drawn = base * np.exp(spread * noise) if base else spread * noise
        out[name] = jnp.asarray(drawn.astype(out[name].dtype))
    for name, factor in factors.items():
        out[name] = (out[name] * factor).astype(out[name].dtype)
    return out
```

```python
from contextlib import ExitStack

import concourse.bass as bass
from concourse import mybir

P = 128
F32 = mybir.dt.float32
F32R = mybir.dt.float32r
F16 = mybir.dt.float16
ALU = mybir.AluOpType
ACT = mybir.ActivationFunctionType
AX_X = mybir.AxisListType.X

BATCH, SEQ, HID = 8, 256, 512
TOKENS = BATCH * SEQ
HEADS, DH = 16, 128
INNER = 2048
KT = HID // P
FT = INNER // P
GT = 512
GROUPS = TOKENS // GT
TILES = TOKENS // P
BT = SEQ // P
PROJ = 4
UNITS = HEADS * GROUPS
CHUNKS = 16
CW = KT * INNER * 2 // CHUNKS
LN_EPS = 1e-5
FFN_EPS = 1e-6
RMS_EPS = 1.1920928955078125e-07
Q_B = 128.0
NEG_BIG = -1e38
SQ = SEQ + 1


def decoder_layer(nc, x_t, x_rows, ctx_t, w_heads, slopes, norm_w, decay, first, w_ffn, out):
    with ExitStack() as ctx:
        def sem(name):
            return ctx.enter_context(nc.semaphore(name))

        def sb(name, shape, dt=F32, stack=ctx):
            return stack.enter_context(nc.sbuf_tensor(name, shape, dt))

        bank = [ctx.enter_context(nc.psum_tensor(f"bank{i}", [P, 512], F32)) for i in range(8)]

        resid = sb("resid", [P, TILES, HID])
        tern = sb("tern", [P, CHUNKS, CW], F16)
        ident = sb("ident", [P, P])
        ones = sb("ones", [P, P])
        neg_half = sb("neg_half", [P, TILES])
        neg_slope = sb("neg_slope", [P, HEADS])
        normw = sb("normw", [P, HEADS])
        dec = sb("dec", [P, KT])
        fst = sb("fst", [P, KT])
        slope_in = sb("slope_in", [P, HEADS])
        wneg = sb("wneg", [P, KT])
        abs_sum = sb("abs_sum", [P, CHUNKS])
        abs_two = sb("abs_two", [P, 2])
        thr = sb("thr", [P, 2, CHUNKS])
        wscale = sb("wscale", [P, 2])
        rms_in = sb("rms_in", [P, TILES])
        rms = sb("rms", [P, TILES])
        inv_qb = 1.0 / Q_B

        att = ExitStack()
        x_hi = sb("x_hi", [P, GROUPS, KT, GT], F32R, att)
        x_lo = sb("x_lo", [P, GROUPS, KT, GT], F32R, att)
        raw = sb("raw", [P, PROJ, HID], F32, att)
        w_hi = sb("w_hi", [P, PROJ, KT, DH], F32R, att)
        w_lo = sb("w_lo", [P, PROJ, KT, DH], F32R, att)
        wo_hi = sb("wo_hi", [P, HID], F32R, att)
        wo_lo = sb("wo_lo", [P, HID], F32R, att)
        decays = sb("decays", [P, HEADS, SEQ], F32, att)
        q_t = sb("q_t", [P, GT], F32, att)
        k_t = sb("k_t", [P, GT], F32, att)
        v_t = sb("v_t", [P, GT], F32, att)
        v_r = sb("v_r", [P, KT, P], F32, att)
        g_t = sb("g_t", [P, GT], F32, att)
        probs = sb("probs", [P, 2, 3 * P], F32, att)
        gated = sb("gated", [P, GT], F32, att)
        u_hi = sb("u_hi", [P, GT], F32R, att)
        u_lo = sb("u_lo", [P, GT], F32R, att)
        o_sq = sb("o_sq", [P, GT], F32, att)
        sq_sum = sb("sq_sum", [P, GROUPS, GT], F32, att)
        w_raw = sb("w_raw", [P, CW], F32, att)
        dist = gated[:, 0:SEQ]
        dist_i = o_sq[:, 0:SEQ].bitcast(mybir.dt.int32)
        att.close()

        ffn = ExitStack()
        x_in = sb("x_in", [P, BT, HID], F32, ffn)
        val = sb("val", [P, KT, SEQ], F32, ffn)
        key = sb("key", [P, KT, SEQ], F32, ffn)
        wfull = sb("wfull", [P, KT, SEQ], F32, ffn)
        pp = sb("pp", [P, KT, SQ], F32, ffn)
        aa = sb("aa", [P, KT, SQ], F32, ffn)
        bb = sb("bb", [P, KT, SQ], F32, ffn)
        e1b = sb("e1b", [P, KT, SEQ], F32, ffn)
        e2b = sb("e2b", [P, KT, SEQ], F32, ffn)
        e1 = sb("e1", [P, KT, SEQ], F32, ffn)
        e2 = sb("e2", [P, KT, SEQ], F32, ffn)
        t1 = sb("t1", [P, KT, SEQ], F32, ffn)
        t2 = sb("t2", [P, KT, SEQ], F32, ffn)
        t3 = sb("t3", [P, KT, SEQ], F32, ffn)
        x1 = sb("x1", [P, BT, HID], F32, ffn)
        x2 = sb("x2", [P, BT, HID], F32, ffn)
        xq = sb("xq", [P, BT, HID], F32, ffn)
        xq_hi = sb("xq_hi", [P, BT, KT, P], F16, ffn)
        xq_lo = sb("xq_lo", [P, BT, KT, P], F16, ffn)
        hid = sb("hid", [P, BT, INNER], F32, ffn)
        hq_hi = sb("hq_hi", [P, FT, P], F16, ffn)
        hq_lo = sb("hq_lo", [P, FT, P], F16, ffn)
        y_out = sb("y_out", [P, BT, HID], F32, ffn)
        stats = sb("stats", [P, BT, 4, 6], F32, ffn)
        mv = sb("mv", [P, BT, 2], F32, ffn)
        var_e = sb("var_e", [P, BT], F32, ffn)
        rstd = sb("rstd", [P, BT], F32, ffn)
        amax = sb("amax", [P, BT], F32, ffn)
        qs = sb("qs", [P, BT], F32, ffn)
        sc_fc = sb("sc_fc", [P, BT], F32, ffn)
        sc_pr = sb("sc_pr", [P, BT], F32, ffn)
        nmean = sb("nmean", [P, BT], F32, ffn)
        ffn.close()

        small_in = sem("small_in")
        xraw_in = [sem(f"xraw_in{g}") for g in range(GROUPS)]
        wraw_in, woraw_in = sem("wraw_in"), sem("woraw_in")
        fraw_in = sem("fraw_in")
        x_hi_ok, x_lo_ok, x_zeroed = sem("x_hi_ok"), sem("x_lo_ok"), sem("x_zeroed")
        wsplit_hi, wsplit = sem("wsplit_hi"), sem("wsplit")
        wo_scaled, wo_hi_ok, wo_split = sem("wo_scaled"), sem("wo_hi_ok"), sem("wo_split")
        pool_const, dist_ok, dve_const = sem("pool_const"), sem("dist_ok"), sem("dve_const")
        decay_exp, decays_ok, ident_ok = sem("decay_exp"), sem("decays_ok"), sem("ident_ok")
        projected, evacuated = sem("projected"), sem("evacuated")
        scored, masked_off, masked = sem("scored"), sem("masked_off"), sem("masked")
        v_turned, v_ready = sem("v_turned"), sem("v_ready")
        mixed, squared, sq_added = sem("mixed"), sem("squared"), sem("sq_added")
        gate_done, u_hi_ok, u_ok = sem("gate_done"), sem("u_hi_ok"), sem("u_ok")
        y_done, y_added = sem("y_done"), sem("y_added")
        abs_ok, abs_two_ok, gamma_ok = sem("abs_ok"), sem("abs_two_ok"), sem("gamma_ok")
        thr_ok, picked, terned = sem("thr_ok"), sem("picked"), sem("terned")
        sq_total, rms_in_ok, rms_ok = sem("sq_total"), sem("rms_in_ok"), sem("rms_ok")
        xin_in, ctx_in = sem("xin_in"), sem("ctx_in")
        w_ok, states0 = sem("w_ok"), sem("states0")
        dstep = sem("dstep")
        aggregated, var_one, var_ok, rstd_ok = sem("aggregated"), sem("var_one"), sem("var_ok"), sem("rstd_ok")
        x1_ok, x1_turned, key_ok = sem("x1_ok"), sem("x1_turned"), sem("key_ok")
        pp_ok, t1d_ok, kd_ok, e1b_ok, e2d_ok = sem("pp_ok"), sem("t1d_ok"), sem("kd_ok"), sem("e1b_ok"), sem("e2d_ok")
        mn_ok, e_ok, e2b_ok, bv_ok = sem("mn_ok"), sem("e_ok"), sem("e2b_ok"), sem("bv_ok")
        ev_ok, den1_ok, den_ok = sem("ev_ok"), sem("den1_ok"), sem("den_ok")
        scans_ok, r_ok, r_turned, x2_ok = sem("scans_ok"), sem("r_ok"), sem("r_turned"), sem("x2_ok")
        xq_ok, xq_turned, xqh_ok, xql_ok = sem("xq_ok"), sem("xq_turned"), sem("xqh_ok"), sem("xql_ok")
        fc_done, gelu_ok, mean_ok, cent_ok = sem("fc_done"), sem("gelu_ok"), sem("mean_ok"), sem("cent_ok")
        hq_ok, hq_turned, hqh_ok, hql_ok = sem("hq_ok"), sem("hq_turned"), sem("hqh_ok"), sem("hql_ok")
        pr_done, pr_read, scfc_ok, out_ok, stored = sem("pr_done"), sem("pr_read"), sem("scfc_ok"), sem("out_ok"), sem("stored")

        PJ = bank[0:2]
        SC = bank[2:4]
        OT, VT = bank[4], bank[5]
        YB = bank[6:8]
        Q, K, V, G = range(PROJ)

        TR = bank[0:2]
        QT = [bank[2], bank[5]]
        FC = bank[3:5]
        HT = bank[5:7]
        PR = [bank[7], bank[2]]

        block = ctx.enter_context(nc.Block())

        def wait(eng, s, value):
            if not isinstance(value, int) or value > 0:
                eng.wait_ge(s, value)

        @block.sync
        def _(sp):
            for dst, src in ((slope_in, slopes), (normw, norm_w), (dec, decay), (fst, first)):
                sp.dma_start(dst[:, :], src).then_inc(small_in, 16)
            sp.dma_start(raw[:, :, :], w_heads[0, :, 0:PROJ, :]).then_inc(wraw_in, 16)
            for g in range(GROUPS):
                sp.dma_start(resid[:, 4 * g:4 * g + 4, :], x_t[:, g, :, :]).then_inc(xraw_in[g], 16)
            sp.wait_ge(wsplit, 1)
            sp.dma_start(raw[:, 0, :], w_heads[0, :, PROJ, :]).then_inc(woraw_in, 16)
            for c in range(CHUNKS):
                wait(sp, abs_ok, c)
                sp.dma_start(w_raw[:, :], w_ffn[c, :, :]).then_inc(fraw_in, 16)
            wait(sp, wsplit, PROJ)
            wait(sp, wo_split, 1)
            sp.dma_start(raw[:, :, :], w_heads[1, :, 0:PROJ, :]).then_inc(wraw_in, 16)
            wait(sp, abs_ok, CHUNKS)
            sp.dma_start(w_raw[:, :], w_ffn[0, :, :]).then_inc(fraw_in, 16)
            with sp.Fori(1, HEADS - 1) as h:
                after = sp.snap(h + 1)
                sp.wait_ge(wsplit, PROJ * h + 1)
                sp.dma_start(raw[:, 0, :], w_heads[h, :, PROJ, :]).then_inc(woraw_in, 16)
                sp.wait_ge(terned, h)
                sp.dma_start(w_raw[:, :], w_ffn[h, :, :]).then_inc(fraw_in, 16)
                sp.wait_ge(wo_split, h + 1)
                sp.dma_start(raw[:, :, :], w_heads[after, :, 0:PROJ, :]).then_inc(wraw_in, 16)
            sp.wait_ge(wsplit, PROJ * (HEADS - 1) + 1)
            sp.dma_start(raw[:, 0, :], w_heads[HEADS - 1, :, PROJ, :]).then_inc(woraw_in, 16)
            sp.wait_ge(terned, HEADS - 1)
            sp.dma_start(w_raw[:, :], w_ffn[HEADS - 1, :, :]).then_inc(fraw_in, 16)
            sp.wait_ge(rms_ok, 1)
            sp.wait_ge(terned, CHUNKS)

            def load_rows(b):
                wait(sp, x1_ok, BT * b)
                sp.dma_start(x_in[:, :, :], x_rows[b, :, :, :]).then_inc(xin_in, 16)

            def load_ctx(b):
                wait(sp, ev_ok, b)
                sp.dma_start(val[:, :, :], ctx_t[b, :, :, :]).then_inc(ctx_in, 16)

            def store(b):
                sp.wait_ge(out_ok, BT * b + BT)
                sp.dma_start(out[b, :, :, :], y_out[:, :, :]).then_inc(stored, 16)

            for b in range(2):
                load_rows(b)
                load_ctx(b)
            store(0)
            with sp.Fori(2, BATCH) as b:
                row_out = sp.snap(b - 1)
                load_rows(b)
                load_ctx(b)
                store(row_out)
            store(BATCH - 1)
            sp.wait_ge(stored, 16 * BATCH)

        @block.tensor
        def _(pe):
            mm = nc.tensor.matmul

            def project(h, g, j):
                n = PROJ * (GROUPS * h + g) + j
                if g == 0:
                    pe.wait_ge(wsplit, PROJ * h + j + 1)
                wait(pe, evacuated, n - 1)
                for kt in range(KT):
                    a, b = w_hi[:, j, kt, :], w_lo[:, j, kt, :]
                    c, d = x_hi[:, g, kt, :], x_lo[:, g, kt, :]
                    mm(PJ[j % 2][:, :], a, c, start=kt == 0, stop=False)
                    mm(PJ[j % 2][:, :], a, d, start=False, stop=False)
                    last = mm(PJ[j % 2][:, :], b, c, start=False, stop=kt == KT - 1)
                last.then_inc(projected, 1)

            def scores(u, b):
                pe.wait_ge(evacuated, PROJ * u + K + 1)
                wait(pe, masked, 2 * u + b - 1)
                o = b * SEQ
                mm(SC[b][:, 0:SEQ], k_t[:, o:o + P], q_t[:, o:o + SEQ], start=True, stop=True)
                mm(SC[b][:, SEQ:SEQ + P], k_t[:, o + P:o + SEQ], q_t[:, o + P:o + SEQ],
                   start=True, stop=True).then_inc(scored, 1)

            def mix(u):
                pe.wait_ge(v_ready, u + 1)
                wait(pe, squared, u)
                for b in range(2):
                    pe.wait_ge(masked, 2 * u + b + 1)
                    o = b * SEQ
                    mm(OT[:, o:o + SEQ], v_r[:, 2 * b, :], probs[:, b, 0:SEQ], start=True, stop=False)
                    last = mm(OT[:, o + P:o + SEQ], v_r[:, 2 * b + 1, :], probs[:, b, SEQ:SEQ + P],
                              start=False, stop=True)
                last.then_inc(mixed, 1)

            def turn_v(u):
                pe.wait_ge(evacuated, PROJ * u + V + 1)
                wait(pe, v_ready, u)
                for t in range(KT):
                    last = nc.tensor.transpose(VT[:, t * P:(t + 1) * P], v_t[:, t * P:(t + 1) * P], ident[:, :])
                last.then_inc(v_turned, 1)

            def output(h, u, tt):
                if tt == 0:
                    pe.wait_ge(u_ok, u + 1)
                    pe.wait_ge(wo_split, h + 1)
                wait(pe, y_added, 4 * u + tt - 1)
                c = slice(tt * P, (tt + 1) * P)
                mm(YB[tt % 2][:, :], u_hi[:, c], wo_hi[:, :], start=True, stop=False)
                mm(YB[tt % 2][:, :], u_hi[:, c], wo_lo[:, :], start=False, stop=False)
                mm(YB[tt % 2][:, :], u_lo[:, c], wo_hi[:, :], start=False, stop=True).then_inc(y_done, 1)

            def unit(h, g, lag1=True, lag2=True):
                u = GROUPS * h + g
                before2 = h if g >= 2 else h - 1
                if lag1:
                    scores(u - 1, 0)
                    scores(u - 1, 1)
                project(h, g, Q)
                if lag2:
                    output(before2, u - 2, 0)
                    output(before2, u - 2, 1)
                project(h, g, K)
                if lag2:
                    output(before2, u - 2, 2)
                    output(before2, u - 2, 3)
                project(h, g, V)
                if lag1:
                    mix(u - 1)
                project(h, g, G)
                turn_v(u)

            pe.wait_ge(ident_ok, 1)
            for g in range(GROUPS):
                pe.wait_ge(x_hi_ok, g + 1)
                pe.wait_ge(x_lo_ok, g + 1)
                unit(0, g, g >= 1, g >= 2)
            pe.wait_ge(abs_two_ok, 1)
            pe.wait_ge(masked, 2 * (GROUPS - 1))
            mm(SC[0][:, 0:2], ones[:, :], abs_two[:, :], start=True, stop=True).then_inc(gamma_ok, 1)
            pe.wait_ge(thr_ok, 3)
            with pe.Fori(1, HEADS) as h:
                for g in range(GROUPS):
                    unit(h, g)
            U = UNITS
            scores(U - 1, 0)
            scores(U - 1, 1)
            for tt in range(4):
                output(HEADS - 1, U - 2, tt)
            mix(U - 1)
            for tt in range(4):
                output(HEADS - 1, U - 1, tt)
            pe.wait_ge(sq_added, UNITS)
            for t in range(TILES):
                last = mm(PJ[0][:, t:t + 1], sq_sum[:, t // 4, (t % 4) * P:(t % 4 + 1) * P], ones[:, 0:1],
                          start=True, stop=True)
            last.then_inc(sq_total, 1)

            def turn_x1(b):
                pe.wait_ge(x1_ok, BT * b + BT)
                wait(pe, x2_ok, BT * b)
                for ct in range(KT):
                    for t in range(BT):
                        o = (ct % 2) * SEQ + t * P
                        last = nc.tensor.transpose(TR[ct // 2][:, o:o + P], x1[:, t, ct * P:(ct + 1) * P],
                                                   ident[:, :])
                last.then_inc(x1_turned, 1)

            def turn_back(b):
                pe.wait_ge(r_ok, b + 1)
                pe.wait_ge(key_ok, 2 * b + 2)
                for t in range(BT):
                    for ct in range(KT):
                        last = nc.tensor.transpose(TR[t][:, ct * P:(ct + 1) * P], t3[:, ct, t * P:(t + 1) * P],
                                                   ident[:, :])
                last.then_inc(r_turned, 1)

            def turn_xq(b, t):
                pe.wait_ge(xq_ok, BT * b + t + 1)
                wait(pe, pr_read, BT * b)
                for kt in range(KT):
                    last = nc.tensor.transpose(QT[t][:, kt * P:(kt + 1) * P], xq[:, t, kt * P:(kt + 1) * P],
                                               ident[:, :])
                last.then_inc(xq_turned, 1)

            def fc(b, t):
                n = BT * b + t
                pe.wait_ge(xqh_ok, n + 1)
                pe.wait_ge(xql_ok, n + 1)
                for f in range(4):
                    wait(pe, gelu_ok, 4 * n + f - 1)
                    for kt in range(KT):
                        c = kt * INNER + f * 512
                        w = tern[:, c // CW, c % CW:c % CW + 512]
                        mm(FC[f % 2][:, :], xq_hi[:, t, kt, :], w, start=kt == 0, stop=False)
                        last = mm(FC[f % 2][:, :], xq_lo[:, t, kt, :], w, start=False, stop=kt == KT - 1)
                    last.then_inc(fc_done, 1)

            def proj(b, t):
                n = BT * b + t
                pe.wait_ge(hq_ok, n + 1)
                for j in range(4):
                    wait(pe, hql_ok, 4 * n + j - 1)
                    for i in range(4):
                        k = 4 * j + i
                        last = nc.tensor.transpose(HT[j % 2][:, i * P:(i + 1) * P], hid[:, t, k * P:(k + 1) * P],
                                                   ident[:, :])
                    last.then_inc(hq_turned, 1)
                wait(pe, pr_read, BT * b)
                for j in range(4):
                    pe.wait_ge(hqh_ok, 4 * n + j + 1)
                    pe.wait_ge(hql_ok, 4 * n + j + 1)
                    for i in range(4):
                        k = 4 * j + i
                        c = KT * INNER + k * HID
                        w = tern[:, c // CW, c % CW:c % CW + HID]
                        mm(PR[t][:, :], hq_hi[:, k, :], w, start=k == 0, stop=False)
                        last = mm(PR[t][:, :], hq_lo[:, k, :], w, start=False, stop=k == FT - 1)
                last.then_inc(pr_done, 1)

            turn_x1(0)
            turn_back(0)
            pe.wait_ge(terned, CHUNKS)

            def row(b):
                for t in range(BT):
                    turn_xq(b, t)
                for t in range(BT):
                    fc(b, t)
                turn_x1(b + 1)
                for t in range(BT):
                    proj(b, t)
                turn_back(b + 1)

            row(0)
            with pe.Fori(1, BATCH - 1) as b:
                row(b)
            for t in range(BT):
                turn_xq(BATCH - 1, t)
            for t in range(BT):
                fc(BATCH - 1, t)
            for t in range(BT):
                proj(BATCH - 1, t)

        @block.scalar
        def _(act):
            fn = nc.scalar.activation

            act.wait_ge(dist_ok, 2)
            act.wait_ge(dve_const, 1)
            for h in range(HEADS):
                fn(decays[:, h, :], dist, ACT.Exp, scale=neg_slope[:, h:h + 1]).then_inc(decay_exp, 1)
            fn(wneg[:, :], dec[:, :], ACT.Exp).then_inc(decay_exp, 1)

            def evacuate(u, j):
                act.wait_ge(projected, PROJ * u + j + 1)
                if j in (Q, K):
                    wait(act, scored, 2 * u)
                    dst = (q_t, k_t)[j][:, :]
                elif j == V:
                    wait(act, v_turned, u)
                    dst = v_t[:, :]
                else:
                    wait(act, gate_done, u)
                    dst = g_t[:, :]
                src = PJ[j % 2][:, :]
                if j == G:
                    fn(dst, src, ACT.Tanh, scale=0.5).then_inc(evacuated, 1)
                else:
                    fn(dst, src, ACT.Silu).then_inc(evacuated, 1)

            def square(u):
                act.wait_ge(gate_done, u + 1)
                wait(act, sq_added, u)
                fn(o_sq[:, :], OT[:, :], ACT.Square).then_inc(squared, 1)

            def copy_v(u):
                act.wait_ge(v_turned, u + 1)
                wait(act, mixed, u)
                fn(v_r[:, :, :], VT[:, :].rearrange("p (a b) -> p a b", a=KT), ACT.Copy).then_inc(v_ready, 1)

            def unit(h, g, lag1=True):
                u = GROUPS * h + g
                for j in (Q, K, V):
                    evacuate(u, j)
                if lag1:
                    square(u - 1)
                evacuate(u, G)
                copy_v(u)

            for g in range(GROUPS):
                act.wait_ge(xraw_in[g], 16)
                fn(x_hi[:, g, :, :], resid[:, 4 * g:4 * g + 4, :], ACT.Copy).then_inc(x_hi_ok, 1)
                unit(0, g, g >= 1)
            with act.Fori(1, HEADS) as h:
                for g in range(GROUPS):
                    unit(h, g)
            square(UNITS - 1)

            def copy_key(b):
                act.wait_ge(x1_turned, b + 1)
                wait(act, r_ok, b)
                for c in range(2):
                    fn(key[:, 2 * c:2 * c + 2, :], TR[c][:, :].rearrange("p (a b) -> p a b", a=2),
                       ACT.Copy).then_inc(key_ok, 1)

            def exps(b):
                act.wait_ge(t1d_ok, b + 1)
                for c in range(KT):
                    fn(e1b[:, c, :], t1[:, c, :], ACT.Exp, bias=wneg[:, c:c + 1]).then_inc(e1b_ok, 1)
                act.wait_ge(e2d_ok, b + 1)
                fn(e2b[:, :, :], e2b[:, :, :], ACT.Exp).then_inc(e2b_ok, 1)
                act.wait_ge(mn_ok, b + 1)
                fn(e2[:, :, :], e2[:, :, :], ACT.Exp).then_inc(e_ok, 1)
                fn(e1[:, :, :], e1[:, :, :], ACT.Exp, scale=-1.0).then_inc(e_ok, 1)

            def split_xq(b, t):
                act.wait_ge(xq_turned, BT * b + t + 1)
                wait(act, fc_done, 4 * (BT * b + t - 1))
                fn(xq_hi[:, t, :, :], QT[t][:, :].rearrange("p (a b) -> p a b", a=KT), ACT.Copy).then_inc(xqh_ok, 1)

            def gelus(b, t):
                n = BT * b + t
                act.wait_ge(scfc_ok, b + 1)
                wait(act, pr_done, n - 1)
                for f in range(4):
                    act.wait_ge(fc_done, 4 * n + f + 1)
                    fn(hid[:, t, f * 512:(f + 1) * 512], FC[f % 2][:, :], ACT.Gelu,
                       scale=sc_fc[:, t:t + 1]).then_inc(gelu_ok, 1)

            def centre(b, t):
                act.wait_ge(mean_ok, b + 1)
                fn(hid[:, t, :], hid[:, t, :], ACT.Identity, bias=nmean[:, t:t + 1]).then_inc(cent_ok, 1)

            def split_hq(b, t):
                n = BT * b + t
                wait(act, pr_done, n)
                for j in range(4):
                    act.wait_ge(hq_turned, 4 * n + j + 1)
                    fn(hq_hi[:, 4 * j:4 * j + 4, :], HT[j % 2][:, :].rearrange("p (a b) -> p a b", a=4),
                       ACT.Copy).then_inc(hqh_ok, 1)

            act.wait_ge(w_ok, 1)
            copy_key(0)
            exps(0)

            def row(b):
                for t in range(BT):
                    split_xq(b, t)
                for t in range(BT):
                    gelus(b, t)
                copy_key(b + 1)
                exps(b + 1)
                for t in range(BT):
                    centre(b, t)
                for t in range(BT):
                    split_hq(b, t)

            row(0)
            with act.Fori(1, BATCH - 1) as b:
                row(b)
            for t in range(BT):
                split_xq(BATCH - 1, t)
            for t in range(BT):
                gelus(BATCH - 1, t)
            for t in range(BT):
                centre(BATCH - 1, t)
            for t in range(BT):
                split_hq(BATCH - 1, t)

        @block.vector
        def _(dve):
            v = nc.vector
            stt, tt, ts = v.scalar_tensor_tensor, v.tensor_tensor, v.tensor_scalar

            def split_w(h, j):
                dve.wait_ge(wraw_in, 16 * h + 16)
                wait(dve, projected, PROJ * (GROUPS * h - 1) + j + 1)
                k = PROJ * h + j + 1
                v.tensor_copy(w_hi[:, j, :, :], raw[:, j, :].rearrange("p (a b) -> p a b", a=KT)).then_inc(wsplit_hi, 1)
                dve.wait_ge(wsplit_hi, k)
                tt(w_lo[:, j, :, :], raw[:, j, :].rearrange("p (a b) -> p a b", a=KT),
                   w_hi[:, j, :, :].bitcast(F32), ALU.subtract).then_inc(wsplit, 1)

            def split_wo(h):
                dve.wait_ge(woraw_in, 16 * h + 16)
                wait(dve, y_done, 4 * GROUPS * h)
                ts(raw[:, 0, :], raw[:, 0, :], normw[:, bass.ds(h, 1)], 0.5, ALU.mult, ALU.mult).then_inc(wo_scaled, 1)
                dve.wait_ge(wo_scaled, h + 1)
                v.tensor_copy(wo_hi[:, :], raw[:, 0, :]).then_inc(wo_hi_ok, 1)
                dve.wait_ge(wo_hi_ok, h + 1)
                tt(wo_lo[:, :], raw[:, 0, :], wo_hi[:, :].bitcast(F32), ALU.subtract).then_inc(wo_split, 1)

            def mask(h, u, b):
                dve.wait_ge(scored, 2 * u + b + 1)
                wait(dve, mixed, u)
                hh = bass.ds(h, 1)
                tt(probs[:, b, 0:SEQ], SC[b][:, 0:SEQ], decays[:, hh, :], ALU.mult).then_inc(masked_off, 1)
                tt(probs[:, b, SEQ:SEQ + P], SC[b][:, SEQ:SEQ + P], decays[:, hh, 0:P], ALU.mult).then_inc(masked, 1)

            def add_y(u, g, t):
                dve.wait_ge(y_done, 4 * u + t + 1)
                if t == 0:
                    wait(dve, y_added, 4 * u)
                tt(resid[:, 4 * g + t, :], resid[:, 4 * g + t, :], YB[t % 2][:, :], ALU.add).then_inc(y_added, 1)

            def gate(u):
                dve.wait_ge(mixed, u + 1)
                dve.wait_ge(evacuated, PROJ * u + G + 1)
                stt(gated[:, :], g_t[:, :], 1.0, OT[:, :], ALU.add, ALU.mult).then_inc(gate_done, 1)
                wait(dve, y_done, 4 * u)
                dve.wait_ge(gate_done, u + 1)
                v.tensor_copy(u_hi[:, :], gated[:, :]).then_inc(u_hi_ok, 1)
                dve.wait_ge(u_hi_ok, u + 1)
                tt(u_lo[:, :], gated[:, :], u_hi[:, :].bitcast(F32), ALU.subtract).then_inc(u_ok, 1)

            def unit(h, g, lag1=True, lag2=True):
                u = GROUPS * h + g
                h1 = h if g >= 1 else h - 1
                if lag1:
                    mask(h1, u - 1, 0)
                if lag2:
                    add_y(u - 2, (g - 2) % GROUPS, 0)
                    add_y(u - 2, (g - 2) % GROUPS, 1)
                if lag1:
                    mask(h1, u - 1, 1)
                if lag2:
                    add_y(u - 2, (g - 2) % GROUPS, 2)
                    add_y(u - 2, (g - 2) % GROUPS, 3)
                if lag1:
                    gate(u - 1)

            dve.wait_ge(small_in, 16 * 4)
            ts(neg_slope[:, :], slope_in[:, :], -1.0, None, ALU.mult).then_inc(dve_const, 1)
            split_w(0, Q)

            def tern_abs(c):
                dve.wait_ge(fraw_in, 16 * c + 16)
                v.tensor_reduce(abs_sum[:, c:c + 1], w_raw[:, :], axis=AX_X, op=ALU.add,
                                apply_absolute_value=True).then_inc(abs_ok, 1)

            for g in range(GROUPS):
                dve.wait_ge(x_hi_ok, g + 1)
                tt(x_lo[:, g, :, :], resid[:, 4 * g:4 * g + 4, :], x_hi[:, g, :, :].bitcast(F32),
                   ALU.subtract).then_inc(x_lo_ok, 1)
                if g == 0:
                    for j in (K, V, G):
                        split_w(0, j)
                    split_wo(0)
                if g == 1:
                    dve.wait_ge(decays_ok, HEADS)
                if g >= 2:
                    dve.wait_ge(x_zeroed, g - 1)
                for c in range(4 * g, 4 * g + 4):
                    tern_abs(c)
                unit(0, g, g >= 1, g >= 2)
                if g == GROUPS - 1:
                    for j in (Q, K, V):
                        split_w(1, j)
            dve.wait_ge(x_zeroed, GROUPS)
            dve.wait_ge(abs_ok, CHUNKS)
            v.tensor_reduce(abs_two[:, :], abs_sum[:, :].rearrange("p (a b) -> p a b", a=2), axis=AX_X,
                            op=ALU.add).then_inc(abs_two_ok, 1)
            dve.wait_ge(gamma_ok, 1)
            half_n = 0.5 / (HID * INNER)
            for k in range(2):
                cols = thr[:, k, :].rearrange("p (a b) -> p a b", a=2)
                src = SC[0][:, 0:2].rearrange("p (a b) -> p a b", b=1).broadcast_to([P, 2, CHUNKS // 2])
                sign = (1.0, -1.0)[k]
                ts(cols, src, sign * half_n, sign * 0.5 * FFN_EPS, ALU.mult, ALU.add).then_inc(thr_ok, 1)
            ts(wscale[:, :], SC[0][:, 0:2], -1.0 / (HID * INNER * Q_B), None, ALU.mult).then_inc(thr_ok, 1)
            dve.wait_ge(thr_ok, 3)

            def ternarise(c):
                cc = bass.ds(c, 1)
                dve.wait_ge(fraw_in, 16 * (CHUNKS + c) + 16)
                ts(tern[:, cc, :], w_raw[:, :], thr[:, 0, cc], None, ALU.is_gt).then_inc(picked, 1)
                dve.wait_ge(picked, c + 1)
                stt(tern[:, cc, :], w_raw[:, :], thr[:, 1, cc], tern[:, cc, :], ALU.is_lt, ALU.subtract).then_inc(terned, 1)

            with dve.Fori(1, HEADS - 1) as h:
                for g in range(GROUPS):
                    unit(h, g)
                    if g == 0:
                        split_w(h, G)
                    if g == 1:
                        split_wo(h)
                    if g == 2:
                        ternarise(h - 1)
                    if g == GROUPS - 1:
                        for j in (Q, K, V):
                            split_w(h + 1, j)
            h = HEADS - 1
            for g in range(GROUPS):
                unit(h, g)
                if g == 0:
                    split_w(h, G)
                if g == 1:
                    split_wo(h)
                if g == 2:
                    ternarise(h - 1)
            U = UNITS
            mask(h, U - 1, 0)
            mask(h, U - 1, 1)
            for t in range(4):
                add_y(U - 2, (U - 2) % GROUPS, t)
            gate(U - 1)
            ternarise(CHUNKS - 1)
            for t in range(4):
                add_y(U - 1, (U - 1) % GROUPS, t)
            dve.wait_ge(sq_total, 1)
            ts(rms_in[:, :], PJ[0][:, 0:TILES], 1.0 / INNER, RMS_EPS, ALU.mult, ALU.add).then_inc(rms_in_ok, 1)
            dve.wait_ge(rms_ok, 1)
            dve.wait_ge(y_added, 4 * UNITS)

            class Count:

                def __init__(self):
                    self.base, self.n = 0, 0

                def next(self):
                    self.n += 1
                    return self.base + self.n

                def n_next(self):
                    return self.base + self.n + 1

            steps, norms = Count(), Count()

            def link(ins):
                ins.then_inc(dstep, 1)
                dve.wait_ge(dstep, steps.next())

            def norm(srcs, eps, parts=1):
                for t in range(BT):
                    for f in range(parts):
                        v.bn_stats(stats[:, t, f, :], srcs[t][:, f * 512:(f + 1) * 512]).then_inc(dstep, 1)
                        if t == 1 and f == 0:
                            v.bn_aggr(mv[:, 0, :], stats[:, 0, 0:parts, :]).then_inc(aggregated, 1)
                        dve.wait_ge(dstep, steps.next())
                dve.wait_ge(aggregated, 2 * norms.n_next() - 1)
                ts(var_e[:, 0:1], mv[:, 0, 1:2], eps, None, ALU.add).then_inc(var_one, 1)
                v.bn_aggr(mv[:, 1, :], stats[:, 1, 0:parts, :]).then_inc(aggregated, 1)
                dve.wait_ge(aggregated, 2 * norms.n_next())
                ts(var_e[:, 1:2], mv[:, 1, 1:2], eps, None, ALU.add).then_inc(var_ok, 1)
                dve.wait_ge(rstd_ok, norms.next())

            def input_norm(b):
                dve.wait_ge(xin_in, 16 * b + 16)
                wait(dve, x1_turned, b)
                for t in range(BT):
                    i = bass.ds(BT * b + t, 1)
                    link(stt(x1[:, t, :], resid[:, i, :], rms[:, i], x_in[:, t, :], ALU.mult, ALU.add))
                norm([x1[:, t, :] for t in range(BT)], LN_EPS)
                for t in range(BT):
                    ts(x1[:, t, :], x1[:, t, :], mv[:, t, 0:1], rstd[:, t:t + 1], ALU.subtract,
                       ALU.mult).then_inc(x1_ok, 1)

            def wkv_exponents(b):
                dve.wait_ge(key_ok, 2 * b + 2)
                wait(dve, r_ok, b)
                for c in range(KT):
                    v.tensor_tensor_scan(pp[:, c, 1:SQ], wfull[:, c, :], key[:, c, :], NEG_BIG,
                                         ALU.add, ALU.max).then_inc(pp_ok, 1)
                dve.wait_ge(pp_ok, KT * b + KT)
                tt(e2b[:, :, :], key[:, :, :], pp[:, :, 1:SQ], ALU.subtract).then_inc(e2d_ok, 1)
                dve.wait_ge(kd_ok, b + 1)
                for c in range(KT):
                    link(ts(e2[:, c, :], t2[:, c, :], fst[:, c:c + 1], 0.0, ALU.add, ALU.min))
                    if c < KT - 1:
                        link(ts(e1[:, c, :], t2[:, c, :], fst[:, c:c + 1], 0.0, ALU.add, ALU.max))
                ts(e1[:, KT - 1, :], t2[:, KT - 1, :], fst[:, KT - 1:KT], 0.0, ALU.add, ALU.max).then_inc(mn_ok, 1)

            def wkv_states(b):
                dve.wait_ge(e1b_ok, KT * b + KT)
                dve.wait_ge(e2b_ok, b + 1)
                for c in range(KT):
                    v.tensor_tensor_scan(bb[:, c, 1:SQ], e1b[:, c, :], e2b[:, c, :], 0.0,
                                         ALU.mult, ALU.add).then_inc(scans_ok, 1)
                dve.wait_ge(bv_ok, b + 1)
                for c in range(KT):
                    v.tensor_tensor_scan(aa[:, c, 1:SQ], e1b[:, c, :], t1[:, c, :], 0.0,
                                         ALU.mult, ALU.add).then_inc(scans_ok, 1)
                dve.wait_ge(scans_ok, 2 * KT * (b + 1))
                dve.wait_ge(e_ok, 2 * b + 2)
                wait(dve, r_turned, b)
                link(tt(t3[:, :, :], e1[:, :, :], aa[:, :, 0:SEQ], ALU.mult))
                dve.wait_ge(ev_ok, b + 1)
                link(tt(t3[:, :, :], t3[:, :, :], t2[:, :, :], ALU.add))
                dve.wait_ge(den_ok, b + 1)
                link(v.reciprocal(e1b[:, :, :], e1b[:, :, :]))
                link(tt(t3[:, :, :], t3[:, :, :], e1b[:, :, :], ALU.mult))
                tt(t3[:, :, :], t3[:, :, :], key[:, :, :], ALU.add).then_inc(r_ok, 1)

            def quantise(dst, t, ready):
                link(ts(dst, dst, qs[:, t:t + 1], Q_B, ALU.mult, ALU.min))
                ts(dst, dst, -Q_B, None, ALU.max).then_inc(ready, 1)

            def quant_scales(scale, weight):
                link(v.reciprocal(qs[:, :], amax[:, :]))
                link(ts(qs[:, :], qs[:, :], Q_B, None, ALU.mult))
                link(tt(scale[:, :], amax[:, :], rstd[:, :], ALU.mult))
                ts(scale[:, :], scale[:, :], wscale[:, weight:weight + 1], None, ALU.mult).then_inc(scfc_ok, 1)

            def hidden_input(b):
                dve.wait_ge(r_turned, b + 1)
                norm([TR[t][:, :] for t in range(BT)], LN_EPS)
                for t in range(BT):
                    ts(x2[:, t, :], TR[t][:, :], mv[:, t, 0:1], rstd[:, t:t + 1], ALU.subtract,
                       ALU.mult).then_inc(x2_ok, 1)
                dve.wait_ge(x2_ok, BT * b + BT)
                norm([x2[:, t, :] for t in range(BT)], FFN_EPS)
                for t in range(BT):
                    link(ts(xq[:, t, :], x2[:, t, :], mv[:, t, 0:1], None, ALU.subtract))
                    link(v.tensor_reduce(amax[:, t:t + 1], xq[:, t, :], axis=AX_X, op=ALU.max,
                                         apply_absolute_value=True))
                quant_scales(sc_fc, 0)
                for t in range(BT):
                    quantise(xq[:, t, :], t, xq_ok)
                for t in range(BT):
                    n = BT * b + t
                    dve.wait_ge(xq_turned, n + 1)
                    dve.wait_ge(xqh_ok, n + 1)
                    tt(xq_lo[:, t, :, :], QT[t][:, :].rearrange("p (a b) -> p a b", a=KT), xq_hi[:, t, :, :],
                       ALU.subtract).then_inc(xql_ok, 1)

            def hidden_norm(b):
                dve.wait_ge(gelu_ok, 4 * (BT * b + BT))
                norm([hid[:, t, :] for t in range(BT)], FFN_EPS, 4)
                ts(nmean[:, :], mv[:, :, 0], -1.0, None, ALU.mult).then_inc(mean_ok, 1)

            def hidden_quant(b):
                for t in range(BT):
                    dve.wait_ge(cent_ok, BT * b + t + 1)
                    link(v.tensor_reduce(amax[:, t:t + 1], hid[:, t, :], axis=AX_X, op=ALU.max,
                                         apply_absolute_value=True))
                quant_scales(sc_pr, 1)
                for t in range(BT):
                    quantise(hid[:, t, :], t, hq_ok)
                for t in range(BT):
                    for j in range(4):
                        k = 4 * (BT * b + t) + j + 1
                        dve.wait_ge(hq_turned, k)
                        dve.wait_ge(hqh_ok, k)
                        tt(hq_lo[:, 4 * j:4 * j + 4, :], HT[j % 2][:, :].rearrange("p (a b) -> p a b", a=4),
                           hq_hi[:, 4 * j:4 * j + 4, :], ALU.subtract).then_inc(hql_ok, 1)

            def result(b):
                wait(dve, stored, 16 * b)
                dve.wait_ge(scfc_ok, 2 * b + 2)
                for t in range(BT):
                    dve.wait_ge(pr_done, BT * b + t + 1)
                    stt(y_out[:, t, :], PR[t][:, :], sc_pr[:, t:t + 1], x2[:, t, :], ALU.mult,
                        ALU.add).then_inc(pr_read, 1)
                dve.wait_ge(pr_read, BT * b + BT)
                norm([y_out[:, t, :] for t in range(BT)], LN_EPS)
                for t in range(BT):
                    ts(y_out[:, t, :], y_out[:, t, :], mv[:, t, 0:1], rstd[:, t:t + 1], ALU.subtract,
                       ALU.mult).then_inc(out_ok, 1)

            def row(b):
                hidden_input(b)
                input_norm(b + 1)
                wkv_exponents(b + 1)
                hidden_norm(b)
                wkv_states(b + 1)
                hidden_quant(b)
                result(b)

            dve.wait_ge(decay_exp, HEADS + 1)
            ts(wneg[:, :], wneg[:, :], -1.0, None, ALU.mult).then_inc(w_ok, 1)
            link(v.memset(wfull[:, :, :], 0.0))
            for c in range(KT):
                link(ts(wfull[:, c, :], wfull[:, c, :], wneg[:, c:c + 1], None, ALU.add))
            dve.wait_ge(states0, 3)
            input_norm(0)
            wkv_exponents(0)
            wkv_states(0)
            s0, n0 = steps.n, norms.n
            row(0)
            ds, dn = steps.n - s0, norms.n - n0
            s1, n1 = steps.n, norms.n
            with dve.Fori(1, BATCH - 1) as b:
                steps.base, steps.n = ds * (b - 1) + s1, 0
                norms.base, norms.n = dn * (b - 1) + n1, 0
                row(b)
                assert steps.n == ds and norms.n == dn
            steps.base, steps.n = ds * (BATCH - 2) + s1, 0
            norms.base, norms.n = dn * (BATCH - 2) + n1, 0
            b = BATCH - 1
            hidden_input(b)
            hidden_norm(b)
            hidden_quant(b)
            result(b)

        @block.gpsimd
        def _(pool):
            g_ = nc.gpsimd
            g_.memset(ident[:, :], 0.0).then_inc(pool_const, 1)
            g_.memset(ones[:, :], 1.0).then_inc(pool_const, 1)
            g_.memset(neg_half[:, :], -0.5).then_inc(pool_const, 1)
            g_.memset(sq_sum[:, :, :], 0.0).then_inc(pool_const, 1)
            g_.iota(dist_i, [[1, SEQ]], 0, -1).then_inc(dist_ok, 1)
            pool.wait_ge(dist_ok, 1)
            g_.tensor_scalar(dist, dist_i, 0.0, None, ALU.max).then_inc(dist_ok, 1)
            pool.wait_ge(pool_const, 4)
            g_.affine_select(out=ident[:, :], in_=ident[:, :], compare_op=ALU.not_equal, fill=1.0, base=0,
                             pattern=[[-1, P]], channel_multiplier=1).then_inc(ident_ok, 1)
            for h in range(HEADS):
                pool.wait_ge(decay_exp, h + 1)
                d = decays[:, h, 0:P]
                g_.affine_select(out=d, in_=d, compare_op=ALU.is_ge, fill=0.0, base=0, pattern=[[1, P]],
                                 channel_multiplier=-1).then_inc(decays_ok, 1)

            def clear(g):
                pool.wait_ge(x_lo_ok, g + 1)
                g_.memset(resid[:, 4 * g:4 * g + 4, :], 0.0).then_inc(x_zeroed, 1)

            def add_squares(u, g):
                pool.wait_ge(squared, u + 1)
                wait(pool, sq_added, u - GROUPS + 1)
                g_.tensor_tensor(sq_sum[:, g, :], sq_sum[:, g, :], o_sq[:, :], ALU.add).then_inc(sq_added, 1)

            clear(0)
            for g in range(1, GROUPS):
                clear(g)
                add_squares(g - 1, g - 1)
            add_squares(GROUPS - 1, GROUPS - 1)
            with pool.Fori(1, HEADS) as h:
                for g in range(GROUPS):
                    add_squares(GROUPS * h + g, g)
            pool.wait_ge(rms_in_ok, 1)
            g_.tensor_tensor(rms[:, :], rms_in[:, :], neg_half[:, :], ALU.pow).then_inc(rms_ok, 1)

            pool.wait_ge(rms_ok, 1)
            g_.memset(pp[:, :, 0:1], NEG_BIG).then_inc(states0, 1)
            g_.memset(aa[:, :, 0:1], 0.0).then_inc(states0, 1)
            g_.memset(bb[:, :, 0:1], 0.0).then_inc(states0, 1)
            pool.wait_ge(states0, 3)

            def root(n):
                pool.wait_ge(var_ok, n)
                g_.tensor_tensor(rstd[:, :], var_e[:, :], neg_half[:, 0:BT], ALU.pow).then_inc(rstd_ok, 1)

            def differences(b):
                pool.wait_ge(pp_ok, KT * b + KT)
                g_.tensor_tensor(t1[:, :, :], pp[:, :, 0:SEQ], pp[:, :, 1:SQ], ALU.subtract).then_inc(t1d_ok, 1)
                g_.tensor_tensor(t2[:, :, :], key[:, :, :], pp[:, :, 0:SEQ], ALU.subtract).then_inc(kd_ok, 1)

            def products(b):
                pool.wait_ge(ctx_in, 16 * b + 16)
                pool.wait_ge(e2b_ok, b + 1)
                pool.wait_ge(e1b_ok, KT * b + KT)
                g_.tensor_tensor(t1[:, :, :], e2b[:, :, :], val[:, :, :], ALU.mult).then_inc(bv_ok, 1)
                pool.wait_ge(e_ok, 2 * b + 2)
                pool.wait_ge(mn_ok, b + 1)
                g_.tensor_tensor(t2[:, :, :], e2[:, :, :], val[:, :, :], ALU.mult).then_inc(ev_ok, 1)
                pool.wait_ge(scans_ok, 2 * KT * (b + 1))
                g_.tensor_tensor(e1b[:, :, :], e1[:, :, :], bb[:, :, 0:SEQ], ALU.mult).then_inc(den1_ok, 1)
                pool.wait_ge(den1_ok, b + 1)
                g_.tensor_tensor(e1b[:, :, :], e1b[:, :, :], e2[:, :, :], ALU.add).then_inc(den_ok, 1)

            root(1)
            differences(0)
            products(0)

            def row(b, n):
                root(n + 1)
                root(n + 2)
                root(n + 3)
                differences(b + 1)
                root(n + 4)
                products(b + 1)
                root(n + 5)

            row(0, 1)
            with pool.Fori(1, BATCH - 1) as b:
                row(b, 5 * b + 1)
            for k in range(4):
                root(5 * (BATCH - 1) + 2 + k)


def kernel(x, ctx_2048, L0_attn_slope_rate, L0_attn_Wqkv, L0_attn_Wg, L0_attn_norm_w, L0_attn_Wo,
           L0_xattn_time_decay, L0_xattn_time_first, L0_ffn_w_fc, L0_ffn_w_proj):
    import numpy as np
    import concourse.bacc as bacc
    from concourse.bass_utils import run_bass_kernel_spmd

    def tiled(w_t):
        return w_t.reshape(-1, P, w_t.shape[1]).transpose(1, 0, 2)

    x = np.asarray(x)
    x_t = tiled(x.reshape(TOKENS, HID).T).reshape(P, KT, GROUPS, GT).transpose(0, 2, 1, 3)
    x_rows = x.reshape(BATCH, BT, P, HID).transpose(0, 2, 1, 3)
    ctx_t = np.asarray(ctx_2048).reshape(BATCH, SEQ, KT, P).transpose(0, 3, 2, 1)
    qkv = np.asarray(L0_attn_Wqkv).reshape(HEADS, 3, DH, KT, P).transpose(0, 4, 1, 3, 2)
    gate = np.asarray(L0_attn_Wg).reshape(HEADS, 1, DH, KT, P).transpose(0, 4, 1, 3, 2)
    wo = np.asarray(L0_attn_Wo).T.reshape(HEADS, P, 1, HID)
    w_heads = np.concatenate([qkv.reshape(HEADS, P, 3, HID), gate.reshape(HEADS, P, 1, HID), wo], axis=2)
    slopes = np.broadcast_to(np.asarray(L0_attn_slope_rate).reshape(1, HEADS), (P, HEADS))
    norm_w = np.asarray(L0_attn_norm_w).reshape(HEADS, P).T
    decay = np.asarray(L0_xattn_time_decay).reshape(KT, P).T
    first = np.asarray(L0_xattn_time_first).reshape(KT, P).T
    w_ffn = np.concatenate([tiled(np.asarray(L0_ffn_w_fc).T).reshape(P, -1),
                            tiled(np.asarray(L0_ffn_w_proj).T).reshape(P, -1)], axis=1)
    w_ffn = w_ffn.reshape(P, CHUNKS, CW).transpose(1, 0, 2)
    laid = {"x_t": x_t, "x_rows": x_rows, "ctx_t": ctx_t, "w_heads": w_heads, "slopes": slopes,
            "norm_w": norm_w, "decay": decay, "first": first, "w_ffn": w_ffn}
    laid = {k: np.ascontiguousarray(a) for k, a in laid.items()}

    nc = bacc.Bacc("TRN2", target_bir_lowering=False, num_devices=1)
    args = {k: nc.dram_tensor(k, a.shape, F32, kind="ExternalInput").ap() for k, a in laid.items()}
    out = nc.dram_tensor("out", (BATCH, P, BT, HID), F32, kind="ExternalOutput").ap()
    decoder_layer(nc, **args, out=out)
    r = run_bass_kernel_spmd(nc, [laid], core_ids=[0])
    got = np.asarray(r.results[0]["out"])
    return got.transpose(0, 2, 1, 3).reshape(BATCH, SEQ, HID)
```

```python
from contextlib import ExitStack

import concourse.bass as bass
from concourse import mybir

P = 128
F32 = mybir.dt.float32
F32R = mybir.dt.float32r
F16 = mybir.dt.float16
ALU = mybir.AluOpType
ACT = mybir.ActivationFunctionType
AX_X = mybir.AxisListType.X

BATCH, SEQ, HID = 8, 256, 512
TOKENS = BATCH * SEQ
HEADS, DH = 16, 128
INNER = 2048
KT = HID // P
FT = INNER // P
GT = 512
GROUPS = TOKENS // GT
TILES = TOKENS // P
BT = SEQ // P
PROJ = 4
UNITS = HEADS * GROUPS
CHUNKS = 16
CW = KT * INNER * 2 // CHUNKS
LN_EPS = 1e-5
FFN_EPS = 1e-6
RMS_EPS = 1.1920928955078125e-07
Q_B = 128.0
NEG_BIG = -1e38
SQ = SEQ + 1


def decoder_layer(nc, x_t, x_rows, ctx_t, w_heads, slopes, norm_w, decay, first, w_ffn, out):
    with ExitStack() as ctx:
        def sem(name):
            return ctx.enter_context(nc.semaphore(name))

        def sb(name, shape, dt=F32, stack=ctx):
            return stack.enter_context(nc.sbuf_tensor(name, shape, dt))

        bank = [ctx.enter_context(nc.psum_tensor(f"bank{i}", [P, 512], F32)) for i in range(8)]

        resid = sb("resid", [P, TILES, HID])
        tern = sb("tern", [P, CHUNKS, CW], F16)
        ident = sb("ident", [P, P])
        ones = sb("ones", [P, P])
        neg_half = sb("neg_half", [P, TILES])
        neg_slope = sb("neg_slope", [P, HEADS])
        normw = sb("normw", [P, HEADS])
        dec = sb("dec", [P, KT])
        fst = sb("fst", [P, KT])
        nfst = sb("nfst", [P, KT])
        slope_in = sb("slope_in", [P, HEADS])
        wneg = sb("wneg", [P, KT])
        abs_sum = sb("abs_sum", [P, CHUNKS])
        abs_two = sb("abs_two", [P, 2])
        thr = sb("thr", [P, 2, CHUNKS])
        wscale = sb("wscale", [P, 2])
        rms_in = sb("rms_in", [P, TILES])
        rms = sb("rms", [P, TILES])
        inv_qb = 1.0 / Q_B

        att = ExitStack()
        x_hi = sb("x_hi", [P, GROUPS, KT, GT], F32R, att)
        x_lo = sb("x_lo", [P, GROUPS, KT, GT], F32R, att)
        raw = sb("raw", [P, PROJ, HID], F32, att)
        w_hi = sb("w_hi", [P, PROJ, KT, DH], F32R, att)
        w_lo = sb("w_lo", [P, PROJ, KT, DH], F32R, att)
        wo_hi = sb("wo_hi", [P, HID], F32R, att)
        wo_lo = sb("wo_lo", [P, HID], F32R, att)
        decays = sb("decays", [P, HEADS, SEQ], F32, att)
        q_t = sb("q_t", [P, GT], F32, att)
        k_t = sb("k_t", [P, GT], F32, att)
        v_t = sb("v_t", [P, GT], F32, att)
        v_r = sb("v_r", [P, KT, P], F32, att)
        g_t = sb("g_t", [P, GT], F32, att)
        probs = sb("probs", [P, 2, 3 * P], F32, att)
        gated = sb("gated", [P, GT], F32, att)
        u_hi = sb("u_hi", [P, GT], F32R, att)
        u_lo = sb("u_lo", [P, GT], F32R, att)
        o_sq = sb("o_sq", [P, GT], F32, att)
        sq_sum = sb("sq_sum", [P, GROUPS, GT], F32, att)
        w_raw = sb("w_raw", [P, CW], F32, att)
        dist = gated[:, 0:SEQ]
        dist_i = o_sq[:, 0:SEQ].bitcast(mybir.dt.int32)
        att.close()

        ffn = ExitStack()
        x_in = sb("x_in", [P, BT, HID], F32, ffn)
        val = sb("val", [P, KT, SEQ], F32, ffn)
        key = sb("key", [P, KT, SEQ], F32, ffn)
        pp = sb("pp", [P, KT, SQ], F32, ffn)
        aa = sb("aa", [P, KT, SQ], F32, ffn)
        bb = sb("bb", [P, KT, SQ], F32, ffn)
        e1b = sb("e1b", [P, KT, SEQ], F32, ffn)
        e2b = sb("e2b", [P, KT, SEQ], F32, ffn)
        e1 = sb("e1", [P, KT, SEQ], F32, ffn)
        e2 = sb("e2", [P, KT, SEQ], F32, ffn)
        t1 = sb("t1", [P, KT, SEQ], F32, ffn)
        t2 = sb("t2", [P, KT, SEQ], F32, ffn)
        num = sb("num", [P, KT, SEQ], F32, ffn)
        den = sb("den", [P, KT, SEQ], F32, ffn)
        x1 = sb("x1", [P, BT, HID], F32, ffn)
        x2 = sb("x2", [P, 2, BT, HID], F32, ffn)
        xq = sb("xq", [P, BT, HID], F32, ffn)
        xq_hi = sb("xq_hi", [P, BT, KT, P], F16, ffn)
        xq_lo = sb("xq_lo", [P, BT, KT, P], F16, ffn)
        hid = sb("hid", [P, BT, INNER], F32, ffn)
        hid_sq = sb("hid_sq", [P, INNER], F32, ffn)
        hq_hi = sb("hq_hi", [P, BT, FT, P], F16, ffn)
        hq_lo = sb("hq_lo", [P, BT, FT, P], F16, ffn)
        y_out = sb("y_out", [P, BT, HID], F32, ffn)
        stats = sb("stats", [P, BT, 6], F32, ffn)
        NORMS = NX, NR, NQ, NH, NO = range(5)
        mv = sb("mv", [P, len(NORMS), BT, 2], F32, ffn)
        var_e = sb("var_e", [P, len(NORMS), BT], F32, ffn)
        rstd = sb("rstd", [P, len(NORMS), BT], F32, ffn)
        amax_x = sb("amax_x", [P, BT], F32, ffn)
        amax_h = sb("amax_h", [P, BT], F32, ffn)
        qs_x = sb("qs_x", [P, BT], F32, ffn)
        qs_h = sb("qs_h", [P, BT], F32, ffn)
        sc_fc = sb("sc_fc", [P, BT], F32, ffn)
        sc_pr = sb("sc_pr", [P, BT], F32, ffn)
        hsum = sb("hsum", [P, BT, 4], F32, ffn)
        hsum_dump = sb("hsum_dump", [P, 4], F32, ffn)
        nmean = sb("nmean", [P, BT], F32, ffn)
        hssq = sb("hssq", [P, BT], F32, ffn)
        ffn.close()

        small_in = sem("small_in")
        xraw_in = [sem(f"xraw_in{g}") for g in range(GROUPS)]
        wraw_in, woraw_in = sem("wraw_in"), sem("woraw_in")
        fraw_in = sem("fraw_in")
        x_hi_ok, x_lo_ok, x_zeroed = sem("x_hi_ok"), sem("x_lo_ok"), sem("x_zeroed")
        wsplit_hi, wsplit = sem("wsplit_hi"), sem("wsplit")
        wo_scaled, wo_hi_ok, wo_split = sem("wo_scaled"), sem("wo_hi_ok"), sem("wo_split")
        pool_const, dist_ok, dve_const = sem("pool_const"), sem("dist_ok"), sem("dve_const")
        decay_exp, decays_ok, ident_ok = sem("decay_exp"), sem("decays_ok"), sem("ident_ok")
        projected, evacuated = sem("projected"), sem("evacuated")
        scored, masked_off, masked = sem("scored"), sem("masked_off"), sem("masked")
        v_turned, v_ready = sem("v_turned"), sem("v_ready")
        mixed, squared, sq_added = sem("mixed"), sem("squared"), sem("sq_added")
        gate_done, u_hi_ok, u_ok = sem("gate_done"), sem("u_hi_ok"), sem("u_ok")
        y_done, y_added = sem("y_done"), sem("y_added")
        abs_ok, abs_two_ok, gamma_ok = sem("abs_ok"), sem("abs_two_ok"), sem("gamma_ok")
        thr_ok, picked, terned = sem("thr_ok"), sem("picked"), sem("terned")
        sq_total, rms_in_ok, rms_ok = sem("sq_total"), sem("rms_in_ok"), sem("rms_ok")
        xin_in, ctx_in = sem("xin_in"), sem("ctx_in")
        w_ok, states0 = sem("w_ok"), sem("states0")
        dstep = sem("dstep")
        var_ok = [sem(f"var_ok{k}") for k in NORMS]
        rstd_ok = [sem(f"rstd_ok{k}") for k in NORMS]
        x1_ok, x1_turned, key_ok = sem("x1_ok"), sem("x1_turned"), sem("key_ok")
        pp_ok, t1d_ok, kd_ok, e1b_ok, e2d_ok = sem("pp_ok"), sem("t1d_ok"), sem("kd_ok"), sem("e1b_ok"), sem("e2d_ok")
        relu_ok, e_ok, e2b_ok, bv_ok = sem("relu_ok"), sem("e_ok"), sem("e2b_ok"), sem("bv_ok")
        ev_ok, den1_ok, den_ok = sem("ev_ok"), sem("den1_ok"), sem("den_ok")
        num1_ok, num_ok = sem("num1_ok"), sem("num_ok")
        scans_ok, r_ok, r_turned, x2_ok = sem("scans_ok"), sem("r_ok"), sem("r_turned"), sem("x2_ok")
        xq_ok, xq_turned, xqh_ok, xql_ok = sem("xq_ok"), sem("xq_turned"), sem("xqh_ok"), sem("xql_ok")
        fc_done, gelu_ok, mean_ok, cent_ok = sem("fc_done"), sem("gelu_ok"), sem("mean_ok"), sem("cent_ok")
        hsq_ok, scpr_ok = sem("hsq_ok"), sem("scpr_ok")
        hq_ok, hq_turned, hqh_ok, hql_ok = sem("hq_ok"), sem("hq_turned"), sem("hqh_ok"), sem("hql_ok")
        pr_done, pr_read, scfc_ok, out_ok, stored = sem("pr_done"), sem("pr_read"), sem("scfc_ok"), sem("out_ok"), sem("stored")

        PJ = bank[0:2]
        SC = bank[2:4]
        OT, VT = bank[4], bank[5]
        YB = bank[6:8]
        Q, K, V, G = range(PROJ)

        TR = bank[0:2]
        FC = bank[3:5]
        QT = bank[5:7]
        HT = bank[3:7]
        PR = [bank[7], bank[2]]

        block = ctx.enter_context(nc.Block())

        def wait(eng, s, value):
            if not isinstance(value, int) or value > 0:
                eng.wait_ge(s, value)

        @block.sync
        def _(sp):
            for dst, src in ((slope_in, slopes), (normw, norm_w), (dec, decay), (fst, first)):
                sp.dma_start(dst[:, :], src).then_inc(small_in, 16)
            sp.dma_start(raw[:, :, :], w_heads[0, :, 0:PROJ, :]).then_inc(wraw_in, 16)
            for g in range(GROUPS):
                sp.dma_start(resid[:, 4 * g:4 * g + 4, :], x_t[:, g, :, :]).then_inc(xraw_in[g], 16)
            sp.wait_ge(wsplit, 1)
            sp.dma_start(raw[:, 0, :], w_heads[0, :, PROJ, :]).then_inc(woraw_in, 16)
            for c in range(CHUNKS):
                wait(sp, abs_ok, c)
                sp.dma_start(w_raw[:, :], w_ffn[c, :, :]).then_inc(fraw_in, 16)
            wait(sp, wsplit, PROJ)
            wait(sp, wo_split, 1)
            sp.dma_start(raw[:, :, :], w_heads[1, :, 0:PROJ, :]).then_inc(wraw_in, 16)
            wait(sp, abs_ok, CHUNKS)
            sp.dma_start(w_raw[:, :], w_ffn[0, :, :]).then_inc(fraw_in, 16)
            with sp.Fori(1, HEADS - 1) as h:
                after = sp.snap(h + 1)
                sp.wait_ge(wsplit, PROJ * h + 1)
                sp.dma_start(raw[:, 0, :], w_heads[h, :, PROJ, :]).then_inc(woraw_in, 16)
                sp.wait_ge(terned, h)
                sp.dma_start(w_raw[:, :], w_ffn[h, :, :]).then_inc(fraw_in, 16)
                sp.wait_ge(wo_split, h + 1)
                sp.dma_start(raw[:, :, :], w_heads[after, :, 0:PROJ, :]).then_inc(wraw_in, 16)
            sp.wait_ge(wsplit, PROJ * (HEADS - 1) + 1)
            sp.dma_start(raw[:, 0, :], w_heads[HEADS - 1, :, PROJ, :]).then_inc(woraw_in, 16)
            sp.wait_ge(terned, HEADS - 1)
            sp.dma_start(w_raw[:, :], w_ffn[HEADS - 1, :, :]).then_inc(fraw_in, 16)
            sp.wait_ge(rms_ok, 1)
            sp.wait_ge(terned, CHUNKS)

            def load_rows(b):
                wait(sp, x1_ok, BT * b)
                sp.dma_start(x_in[:, :, :], x_rows[b, :, :, :]).then_inc(xin_in, 16)

            def load_ctx(b):
                wait(sp, ev_ok, b)
                sp.dma_start(val[:, :, :], ctx_t[b, :, :, :]).then_inc(ctx_in, 16)

            def store(b):
                sp.wait_ge(out_ok, BT * b + BT)
                sp.dma_start(out[b, :, :, :], y_out[:, :, :]).then_inc(stored, 16)

            load_rows(0)
            load_ctx(0)
            load_rows(1)
            load_ctx(1)
            load_rows(2)
            with sp.Fori(1, BATCH - 2) as b:
                ctx_row, x_row, row_out = sp.snap(b + 1), sp.snap(b + 2), sp.snap(b - 1)
                load_ctx(ctx_row)
                load_rows(x_row)
                store(row_out)
            load_ctx(BATCH - 1)
            for b in range(BATCH - 3, BATCH):
                store(b)
            sp.wait_ge(stored, 16 * BATCH)

        @block.tensor
        def _(pe):
            mm = nc.tensor.matmul

            def project(h, g, j):
                n = PROJ * (GROUPS * h + g) + j
                if g == 0:
                    pe.wait_ge(wsplit, PROJ * h + j + 1)
                wait(pe, evacuated, n - 1)
                for kt in range(KT):
                    a, b = w_hi[:, j, kt, :], w_lo[:, j, kt, :]
                    c, d = x_hi[:, g, kt, :], x_lo[:, g, kt, :]
                    mm(PJ[j % 2][:, :], a, c, start=kt == 0, stop=False)
                    mm(PJ[j % 2][:, :], a, d, start=False, stop=False)
                    last = mm(PJ[j % 2][:, :], b, c, start=False, stop=kt == KT - 1)
                last.then_inc(projected, 1)

            def scores(u, b):
                pe.wait_ge(evacuated, PROJ * u + K + 1)
                wait(pe, masked, 2 * u + b - 1)
                o = b * SEQ
                mm(SC[b][:, 0:SEQ], k_t[:, o:o + P], q_t[:, o:o + SEQ], start=True, stop=True)
                mm(SC[b][:, SEQ:SEQ + P], k_t[:, o + P:o + SEQ], q_t[:, o + P:o + SEQ],
                   start=True, stop=True).then_inc(scored, 1)

            def mix(u):
                pe.wait_ge(v_ready, u + 1)
                wait(pe, squared, u)
                for b in range(2):
                    pe.wait_ge(masked, 2 * u + b + 1)
                    o = b * SEQ
                    mm(OT[:, o:o + SEQ], v_r[:, 2 * b, :], probs[:, b, 0:SEQ], start=True, stop=False)
                    last = mm(OT[:, o + P:o + SEQ], v_r[:, 2 * b + 1, :], probs[:, b, SEQ:SEQ + P],
                              start=False, stop=True)
                last.then_inc(mixed, 1)

            def turn_v(u):
                pe.wait_ge(evacuated, PROJ * u + V + 1)
                wait(pe, v_ready, u)
                for t in range(KT):
                    last = nc.tensor.transpose(VT[:, t * P:(t + 1) * P], v_t[:, t * P:(t + 1) * P], ident[:, :])
                last.then_inc(v_turned, 1)

            def output(h, u, tt):
                if tt == 0:
                    pe.wait_ge(u_ok, u + 1)
                    pe.wait_ge(wo_split, h + 1)
                wait(pe, y_added, 4 * u + tt - 1)
                c = slice(tt * P, (tt + 1) * P)
                mm(YB[tt % 2][:, :], u_hi[:, c], wo_hi[:, :], start=True, stop=False)
                mm(YB[tt % 2][:, :], u_hi[:, c], wo_lo[:, :], start=False, stop=False)
                mm(YB[tt % 2][:, :], u_lo[:, c], wo_hi[:, :], start=False, stop=True).then_inc(y_done, 1)

            def unit(h, g, lag1=True, lag2=True):
                u = GROUPS * h + g
                before2 = h if g >= 2 else h - 1
                if lag1:
                    scores(u - 1, 0)
                    scores(u - 1, 1)
                project(h, g, Q)
                if lag2:
                    output(before2, u - 2, 0)
                    output(before2, u - 2, 1)
                project(h, g, K)
                if lag2:
                    output(before2, u - 2, 2)
                    output(before2, u - 2, 3)
                project(h, g, V)
                if lag1:
                    mix(u - 1)
                project(h, g, G)
                turn_v(u)

            pe.wait_ge(ident_ok, 1)
            for g in range(GROUPS):
                pe.wait_ge(x_hi_ok, g + 1)
                pe.wait_ge(x_lo_ok, g + 1)
                unit(0, g, g >= 1, g >= 2)
            pe.wait_ge(abs_two_ok, 1)
            pe.wait_ge(masked, 2 * (GROUPS - 1))
            mm(SC[0][:, 0:2], ones[:, :], abs_two[:, :], start=True, stop=True).then_inc(gamma_ok, 1)
            pe.wait_ge(thr_ok, 3)
            with pe.Fori(1, HEADS) as h:
                for g in range(GROUPS):
                    unit(h, g)
            U = UNITS
            scores(U - 1, 0)
            scores(U - 1, 1)
            for tt in range(4):
                output(HEADS - 1, U - 2, tt)
            mix(U - 1)
            for tt in range(4):
                output(HEADS - 1, U - 1, tt)
            pe.wait_ge(sq_added, UNITS)
            for t in range(TILES):
                last = mm(PJ[0][:, t:t + 1], sq_sum[:, t // 4, (t % 4) * P:(t % 4 + 1) * P], ones[:, 0:1],
                          start=True, stop=True)
            last.then_inc(sq_total, 1)

            def turn_x1(b):
                pe.wait_ge(x1_ok, BT * b + BT)
                wait(pe, x2_ok, BT * b)
                for ct in range(KT):
                    for t in range(BT):
                        o = (ct % 2) * SEQ + t * P
                        last = nc.tensor.transpose(TR[ct // 2][:, o:o + P], x1[:, t, ct * P:(ct + 1) * P],
                                                   ident[:, :])
                last.then_inc(x1_turned, 1)

            def turn_back(b):
                pe.wait_ge(r_ok, b + 1)
                pe.wait_ge(key_ok, 2 * b + 2)
                for t in range(BT):
                    for ct in range(KT):
                        last = nc.tensor.transpose(TR[t][:, ct * P:(ct + 1) * P], num[:, ct, t * P:(t + 1) * P],
                                                   ident[:, :])
                last.then_inc(r_turned, 1)

            def turn_xq(b, t):
                pe.wait_ge(xq_ok, BT * b + t + 1)
                wait(pe, hql_ok, 4 * BT * b)
                for kt in range(KT):
                    last = nc.tensor.transpose(QT[t][:, kt * P:(kt + 1) * P], xq[:, t, kt * P:(kt + 1) * P],
                                               ident[:, :])
                last.then_inc(xq_turned, 1)

            def fc(b, t):
                n = BT * b + t
                pe.wait_ge(xqh_ok, n + 1)
                pe.wait_ge(xql_ok, n + 1)
                for f in range(4):
                    wait(pe, gelu_ok, 4 * n + f - 1)
                    for kt in range(KT):
                        c = kt * INNER + f * 512
                        w = tern[:, c // CW, c % CW:c % CW + 512]
                        mm(FC[f % 2][:, :], xq_hi[:, t, kt, :], w, start=kt == 0, stop=False)
                        last = mm(FC[f % 2][:, :], xq_lo[:, t, kt, :], w, start=False, stop=kt == KT - 1)
                    last.then_inc(fc_done, 1)

            def turn_hq(b, t):
                n = BT * b + t
                pe.wait_ge(gelu_ok, 4 * BT * (b + 1))
                pe.wait_ge(hq_ok, n + 1)
                for j in range(4):
                    if t > 0:
                        pe.wait_ge(hql_ok, 4 * (n - 1) + j + 1)
                    for i in range(4):
                        k = 4 * j + i
                        last = nc.tensor.transpose(HT[j][:, i * P:(i + 1) * P], hid[:, t, k * P:(k + 1) * P],
                                                   ident[:, :])
                    last.then_inc(hq_turned, 1)

            def proj(b, t):
                n = BT * b + t
                pe.wait_ge(hqh_ok, 4 * n + 4)
                pe.wait_ge(hql_ok, 4 * n + 4)
                wait(pe, pr_read, n - 1)
                for k in range(FT):
                    c = KT * INNER + k * HID
                    w = tern[:, c // CW, c % CW:c % CW + HID]
                    mm(PR[t][:, :], hq_hi[:, t, k, :], w, start=k == 0, stop=False)
                    last = mm(PR[t][:, :], hq_lo[:, t, k, :], w, start=False, stop=k == FT - 1)
                last.then_inc(pr_done, 1)

            def row(b, first=False, final=False):
                if not final:
                    turn_x1(b + 1)
                for t in range(BT):
                    turn_xq(b, t)
                if not first:
                    proj(b - 1, 1)
                for t in range(BT):
                    fc(b, t)
                if not final:
                    turn_back(b + 1)
                for t in range(BT):
                    turn_hq(b, t)
                proj(b, 0)

            turn_x1(0)
            turn_back(0)
            pe.wait_ge(terned, CHUNKS)
            row(0, first=True)
            with pe.Fori(1, BATCH - 1) as b:
                row(b)
            row(BATCH - 1, final=True)
            proj(BATCH - 1, 1)

        @block.scalar
        def _(act):
            fn = nc.scalar.activation

            act.wait_ge(dist_ok, 2)
            act.wait_ge(dve_const, 1)
            for h in range(HEADS):
                fn(decays[:, h, :], dist, ACT.Exp, scale=neg_slope[:, h:h + 1]).then_inc(decay_exp, 1)
            fn(wneg[:, :], dec[:, :], ACT.Exp).then_inc(decay_exp, 1)

            def evacuate(u, j):
                act.wait_ge(projected, PROJ * u + j + 1)
                if j in (Q, K):
                    wait(act, scored, 2 * u)
                    dst = (q_t, k_t)[j][:, :]
                elif j == V:
                    wait(act, v_turned, u)
                    dst = v_t[:, :]
                else:
                    wait(act, gate_done, u)
                    dst = g_t[:, :]
                src = PJ[j % 2][:, :]
                if j == G:
                    fn(dst, src, ACT.Tanh, scale=0.5).then_inc(evacuated, 1)
                else:
                    fn(dst, src, ACT.Silu).then_inc(evacuated, 1)

            def square(u):
                act.wait_ge(gate_done, u + 1)
                wait(act, sq_added, u)
                fn(o_sq[:, :], OT[:, :], ACT.Square).then_inc(squared, 1)

            def copy_v(u):
                act.wait_ge(v_turned, u + 1)
                wait(act, mixed, u)
                fn(v_r[:, :, :], VT[:, :].rearrange("p (a b) -> p a b", a=KT), ACT.Copy).then_inc(v_ready, 1)

            def unit(h, g, lag1=True):
                u = GROUPS * h + g
                for j in (Q, K, V):
                    evacuate(u, j)
                if lag1:
                    square(u - 1)
                evacuate(u, G)
                copy_v(u)

            for g in range(GROUPS):
                act.wait_ge(xraw_in[g], 16)
                fn(x_hi[:, g, :, :], resid[:, 4 * g:4 * g + 4, :], ACT.Copy).then_inc(x_hi_ok, 1)
                unit(0, g, g >= 1)
            with act.Fori(1, HEADS) as h:
                for g in range(GROUPS):
                    unit(h, g)
            square(UNITS - 1)

            def copy_key(b):
                act.wait_ge(x1_turned, b + 1)
                wait(act, r_ok, b)
                for c in range(2):
                    fn(key[:, 2 * c:2 * c + 2, :], TR[c][:, :].rearrange("p (a b) -> p a b", a=2),
                       ACT.Copy).then_inc(key_ok, 1)

            def exps(b):
                act.wait_ge(t1d_ok, b + 1)
                for c in range(KT):
                    fn(e1b[:, c, :], t1[:, c, :], ACT.Exp, bias=wneg[:, c:c + 1]).then_inc(e1b_ok, 1)
                act.wait_ge(e2d_ok, b + 1)
                fn(e2b[:, :, :], e2b[:, :, :], ACT.Exp).then_inc(e2b_ok, 1)
                act.wait_ge(kd_ok, b + 1)
                for c in range(KT):
                    fn(e1[:, c, :], t2[:, c, :], ACT.Relu, bias=fst[:, c:c + 1]).then_inc(relu_ok, 1)
                for c in range(KT):
                    fn(e2[:, c, :], t2[:, c, :], ACT.Relu, bias=nfst[:, c:c + 1], scale=-1.0).then_inc(relu_ok, 1)
                act.wait_ge(relu_ok, 2 * KT * (b + 1))
                fn(e1[:, :, :], e1[:, :, :], ACT.Exp, scale=-1.0).then_inc(e_ok, 1)
                fn(e2[:, :, :], e2[:, :, :], ACT.Exp, scale=-1.0).then_inc(e_ok, 1)

            def split_xq(b, t):
                act.wait_ge(xq_turned, BT * b + t + 1)
                fn(xq_hi[:, t, :, :], QT[t][:, :].rearrange("p (a b) -> p a b", a=KT), ACT.Copy).then_inc(xqh_ok, 1)

            def gelu(b, t, f):
                n = BT * b + t
                if f == 0:
                    wait(act, hq_turned, 4 * (n - 1))
                act.wait_ge(fc_done, 4 * n + f + 1)
                fn(hid[:, t, f * 512:(f + 1) * 512], FC[f % 2][:, :], ACT.Gelu, scale=sc_fc[:, t:t + 1],
                   accum_out=hsum[:, t, f:f + 1]).then_inc(gelu_ok, 1)

            def centre(b, t):
                n = BT * b + t
                act.wait_ge(gelu_ok, 4 * n + 4)
                fn(hsum_dump[:, :], hsum[:, t, :], ACT.Identity, scale=-1.0 / INNER,
                   accum_out=nmean[:, t:t + 1]).then_inc(mean_ok, 1)
                act.wait_ge(mean_ok, n + 1)
                fn(hid[:, t, :], hid[:, t, :], ACT.Identity, bias=nmean[:, t:t + 1]).then_inc(cent_ok, 1)

            def variance(b, t):
                n = BT * b + t
                act.wait_ge(cent_ok, n + 1)
                fn(hid_sq[:, :], hid[:, t, :], ACT.Square, accum_out=hssq[:, t:t + 1]).then_inc(hsq_ok, 1)

            def split_hq(b, t):
                n = BT * b + t
                wait(act, pr_done, n - 1)
                for j in range(4):
                    act.wait_ge(hq_turned, 4 * n + j + 1)
                    fn(hq_hi[:, t, 4 * j:4 * j + 4, :], HT[j][:, :].rearrange("p (a b) -> p a b", a=4),
                       ACT.Copy).then_inc(hqh_ok, 1)

            def row(b, final=False):
                if not final:
                    copy_key(b + 1)
                for t in range(BT):
                    split_xq(b, t)
                if not final:
                    exps(b + 1)
                act.wait_ge(scfc_ok, b + 1)
                for f in range(4):
                    gelu(b, 0, f)
                gelu(b, 1, 0)
                centre(b, 0)
                gelu(b, 1, 1)
                variance(b, 0)
                gelu(b, 1, 2)
                gelu(b, 1, 3)
                centre(b, 1)
                variance(b, 1)
                for t in range(BT):
                    split_hq(b, t)

            act.wait_ge(w_ok, 2)
            copy_key(0)
            exps(0)
            row(0)
            with act.Fori(1, BATCH - 1) as b:
                row(b)
            row(BATCH - 1, final=True)

        @block.vector
        def _(dve):
            v = nc.vector
            stt, tt, ts = v.scalar_tensor_tensor, v.tensor_tensor, v.tensor_scalar

            def split_w(h, j):
                dve.wait_ge(wraw_in, 16 * h + 16)
                wait(dve, projected, PROJ * (GROUPS * h - 1) + j + 1)
                k = PROJ * h + j + 1
                v.tensor_copy(w_hi[:, j, :, :], raw[:, j, :].rearrange("p (a b) -> p a b", a=KT)).then_inc(wsplit_hi, 1)
                dve.wait_ge(wsplit_hi, k)
                tt(w_lo[:, j, :, :], raw[:, j, :].rearrange("p (a b) -> p a b", a=KT),
                   w_hi[:, j, :, :].bitcast(F32), ALU.subtract).then_inc(wsplit, 1)

            def split_wo(h):
                dve.wait_ge(woraw_in, 16 * h + 16)
                wait(dve, y_done, 4 * GROUPS * h)
                ts(raw[:, 0, :], raw[:, 0, :], normw[:, bass.ds(h, 1)], 0.5, ALU.mult, ALU.mult).then_inc(wo_scaled, 1)
                dve.wait_ge(wo_scaled, h + 1)
                v.tensor_copy(wo_hi[:, :], raw[:, 0, :]).then_inc(wo_hi_ok, 1)
                dve.wait_ge(wo_hi_ok, h + 1)
                tt(wo_lo[:, :], raw[:, 0, :], wo_hi[:, :].bitcast(F32), ALU.subtract).then_inc(wo_split, 1)

            def mask(h, u, b):
                dve.wait_ge(scored, 2 * u + b + 1)
                wait(dve, mixed, u)
                hh = bass.ds(h, 1)
                tt(probs[:, b, 0:SEQ], SC[b][:, 0:SEQ], decays[:, hh, :], ALU.mult).then_inc(masked_off, 1)
                tt(probs[:, b, SEQ:SEQ + P], SC[b][:, SEQ:SEQ + P], decays[:, hh, 0:P], ALU.mult).then_inc(masked, 1)

            def add_y(u, g, t):
                dve.wait_ge(y_done, 4 * u + t + 1)
                if t == 0:
                    wait(dve, y_added, 4 * u)
                tt(resid[:, 4 * g + t, :], resid[:, 4 * g + t, :], YB[t % 2][:, :], ALU.add).then_inc(y_added, 1)

            def gate(u):
                dve.wait_ge(mixed, u + 1)
                dve.wait_ge(evacuated, PROJ * u + G + 1)
                stt(gated[:, :], g_t[:, :], 1.0, OT[:, :], ALU.add, ALU.mult).then_inc(gate_done, 1)
                wait(dve, y_done, 4 * u)
                dve.wait_ge(gate_done, u + 1)
                v.tensor_copy(u_hi[:, :], gated[:, :]).then_inc(u_hi_ok, 1)
                dve.wait_ge(u_hi_ok, u + 1)
                tt(u_lo[:, :], gated[:, :], u_hi[:, :].bitcast(F32), ALU.subtract).then_inc(u_ok, 1)

            def unit(h, g, lag1=True, lag2=True):
                u = GROUPS * h + g
                h1 = h if g >= 1 else h - 1
                if lag1:
                    mask(h1, u - 1, 0)
                if lag2:
                    add_y(u - 2, (g - 2) % GROUPS, 0)
                    add_y(u - 2, (g - 2) % GROUPS, 1)
                if lag1:
                    mask(h1, u - 1, 1)
                if lag2:
                    add_y(u - 2, (g - 2) % GROUPS, 2)
                    add_y(u - 2, (g - 2) % GROUPS, 3)
                if lag1:
                    gate(u - 1)

            dve.wait_ge(small_in, 16 * 4)
            ts(neg_slope[:, :], slope_in[:, :], -1.0, None, ALU.mult).then_inc(dve_const, 1)
            split_w(0, Q)

            def tern_abs(c):
                dve.wait_ge(fraw_in, 16 * c + 16)
                v.tensor_reduce(abs_sum[:, c:c + 1], w_raw[:, :], axis=AX_X, op=ALU.add,
                                apply_absolute_value=True).then_inc(abs_ok, 1)

            for g in range(GROUPS):
                dve.wait_ge(x_hi_ok, g + 1)
                tt(x_lo[:, g, :, :], resid[:, 4 * g:4 * g + 4, :], x_hi[:, g, :, :].bitcast(F32),
                   ALU.subtract).then_inc(x_lo_ok, 1)
                if g == 0:
                    for j in (K, V, G):
                        split_w(0, j)
                    split_wo(0)
                if g == 1:
                    dve.wait_ge(decays_ok, HEADS)
                if g >= 2:
                    dve.wait_ge(x_zeroed, g - 1)
                for c in range(4 * g, 4 * g + 4):
                    tern_abs(c)
                unit(0, g, g >= 1, g >= 2)
                if g == GROUPS - 1:
                    for j in (Q, K, V):
                        split_w(1, j)
            dve.wait_ge(x_zeroed, GROUPS)
            dve.wait_ge(abs_ok, CHUNKS)
            v.tensor_reduce(abs_two[:, :], abs_sum[:, :].rearrange("p (a b) -> p a b", a=2), axis=AX_X,
                            op=ALU.add).then_inc(abs_two_ok, 1)
            dve.wait_ge(gamma_ok, 1)
            half_n = 0.5 / (HID * INNER)
            for k in range(2):
                cols = thr[:, k, :].rearrange("p (a b) -> p a b", a=2)
                src = SC[0][:, 0:2].rearrange("p (a b) -> p a b", b=1).broadcast_to([P, 2, CHUNKS // 2])
                sign = (1.0, -1.0)[k]
                ts(cols, src, sign * half_n, sign * 0.5 * FFN_EPS, ALU.mult, ALU.add).then_inc(thr_ok, 1)
            ts(wscale[:, :], SC[0][:, 0:2], -1.0 / (HID * INNER * Q_B), None, ALU.mult).then_inc(thr_ok, 1)
            dve.wait_ge(thr_ok, 3)

            def ternarise(c):
                cc = bass.ds(c, 1)
                dve.wait_ge(fraw_in, 16 * (CHUNKS + c) + 16)
                ts(tern[:, cc, :], w_raw[:, :], thr[:, 0, cc], None, ALU.is_gt).then_inc(picked, 1)
                dve.wait_ge(picked, c + 1)
                stt(tern[:, cc, :], w_raw[:, :], thr[:, 1, cc], tern[:, cc, :], ALU.is_lt, ALU.subtract).then_inc(terned, 1)

            with dve.Fori(1, HEADS - 1) as h:
                for g in range(GROUPS):
                    unit(h, g)
                    if g == 0:
                        split_w(h, G)
                    if g == 1:
                        split_wo(h)
                    if g == 2:
                        ternarise(h - 1)
                    if g == GROUPS - 1:
                        for j in (Q, K, V):
                            split_w(h + 1, j)
            h = HEADS - 1
            for g in range(GROUPS):
                unit(h, g)
                if g == 0:
                    split_w(h, G)
                if g == 1:
                    split_wo(h)
                if g == 2:
                    ternarise(h - 1)
            U = UNITS
            mask(h, U - 1, 0)
            mask(h, U - 1, 1)
            for t in range(4):
                add_y(U - 2, (U - 2) % GROUPS, t)
            gate(U - 1)
            ternarise(CHUNKS - 1)
            for t in range(4):
                add_y(U - 1, (U - 1) % GROUPS, t)
            dve.wait_ge(sq_total, 1)
            ts(rms_in[:, :], PJ[0][:, 0:TILES], 1.0 / INNER, RMS_EPS, ALU.mult, ALU.add).then_inc(rms_in_ok, 1)
            dve.wait_ge(rms_ok, 1)
            dve.wait_ge(y_added, 4 * UNITS)

            class Count:

                def __init__(self):
                    self.base, self.n = 0, 0

                def next(self):
                    self.n += 1
                    return self.base + self.n

                def n_next(self):
                    return self.base + self.n + 1

            steps = Count()

            def link(ins):
                ins.then_inc(dstep, 1)
                dve.wait_ge(dstep, steps.next())

            def norm_stats(k, srcs, eps):
                link(v.bn_stats(stats[:, 0, :], srcs[0]))
                v.bn_stats(stats[:, 1, :], srcs[1]).then_inc(dstep, 1)
                steps.next()
                link(v.bn_aggr(mv[:, k, 0, :], stats[:, 0, :]))
                ts(var_e[:, k, 0:1], mv[:, k, 0, 1:2], eps, None, ALU.add).then_inc(dstep, 1)
                steps.next()
                link(v.bn_aggr(mv[:, k, 1, :], stats[:, 1, :]))
                ts(var_e[:, k, 1:2], mv[:, k, 1, 1:2], eps, None, ALU.add).then_inc(var_ok[k], 1)

            def normalise(k, b, t, dst, src, done):
                if t == 0:
                    dve.wait_ge(rstd_ok[k], b + 1)
                ts(dst, src, mv[:, k, t, 0:1], rstd[:, k, t:t + 1], ALU.subtract, ALU.mult).then_inc(done, 1)

            def input_sum(b):
                dve.wait_ge(xin_in, 16 * b + 16)
                wait(dve, x1_turned, b)
                for t in range(BT):
                    i = bass.ds(BT * b + t, 1)
                    link(stt(x1[:, t, :], resid[:, i, :], rms[:, i], x_in[:, t, :], ALU.mult, ALU.add))
                norm_stats(NX, [x1[:, t, :] for t in range(BT)], LN_EPS)

            def input_norm(b):
                for t in range(BT):
                    normalise(NX, b, t, x1[:, t, :], x1[:, t, :], x1_ok)

            def maxima(b):
                dve.wait_ge(key_ok, 2 * b + 2)
                for c in range(KT):
                    v.tensor_tensor_scan(pp[:, c, 1:SQ], wneg[:, c:c + 1].broadcast_to([P, SEQ]), key[:, c, :],
                                         NEG_BIG, ALU.add, ALU.max).then_inc(pp_ok, 1)
                dve.wait_ge(pp_ok, KT * b + KT)
                tt(e2b[:, :, :], key[:, :, :], pp[:, :, 1:SQ], ALU.subtract).then_inc(e2d_ok, 1)

            def states(b):
                dve.wait_ge(e1b_ok, KT * b + KT)
                dve.wait_ge(e2b_ok, b + 1)
                for c in range(KT):
                    v.tensor_tensor_scan(bb[:, c, 1:SQ], e1b[:, c, :], e2b[:, c, :], 0.0,
                                         ALU.mult, ALU.add).then_inc(scans_ok, 1)
                dve.wait_ge(bv_ok, b + 1)
                for c in range(KT):
                    v.tensor_tensor_scan(aa[:, c, 1:SQ], e1b[:, c, :], t1[:, c, :], 0.0,
                                         ALU.mult, ALU.add).then_inc(scans_ok, 1)

            def ratio(b):
                dve.wait_ge(den_ok, b + 1)
                link(v.reciprocal(den[:, :, :], den[:, :, :]))
                dve.wait_ge(num_ok, b + 1)
                link(tt(num[:, :, :], num[:, :, :], den[:, :, :], ALU.mult))
                tt(num[:, :, :], num[:, :, :], key[:, :, :], ALU.add).then_inc(r_ok, 1)

            def r_stats(b):
                dve.wait_ge(r_turned, b + 1)
                norm_stats(NR, [TR[t][:, :] for t in range(BT)], LN_EPS)

            def second_norm(b, s):
                for t in range(BT):
                    normalise(NR, b, t, x2[:, s, t, :], TR[t][:, :], x2_ok)
                dve.wait_ge(x2_ok, BT * b + BT)
                norm_stats(NQ, [x2[:, s, t, :] for t in range(BT)], FFN_EPS)

            def quantise_x(b, s):
                for t in range(BT):
                    link(ts(xq[:, t, :], x2[:, s, t, :], mv[:, NQ, t, 0:1], None, ALU.subtract))
                    link(v.tensor_reduce(amax_x[:, t:t + 1], xq[:, t, :], axis=AX_X, op=ALU.max,
                                         apply_absolute_value=True))
                link(v.reciprocal(qs_x[:, :], amax_x[:, :]))
                link(ts(qs_x[:, :], qs_x[:, :], Q_B, None, ALU.mult))
                for t in range(BT):
                    ts(xq[:, t, :], xq[:, t, :], qs_x[:, t:t + 1], Q_B, ALU.mult, ALU.min).then_inc(xq_ok, 1)

            def split_x(b):
                for t in range(BT):
                    n = BT * b + t
                    dve.wait_ge(xqh_ok, n + 1)
                    stt(xq_lo[:, t, :, :], QT[t][:, :].rearrange("p (a b) -> p a b", a=KT), -Q_B, xq_hi[:, t, :, :],
                        ALU.max, ALU.subtract).then_inc(xql_ok, 1)

            def product_scale(b, k, scale, amax, weight, ready):
                dve.wait_ge(rstd_ok[k], b + 1)
                link(tt(scale[:, :], amax[:, :], rstd[:, k, :], ALU.mult))
                ts(scale[:, :], scale[:, :], wscale[:, weight:weight + 1], None, ALU.mult).then_inc(ready, 1)

            def quantise_hidden(b, t):
                n = BT * b + t
                dve.wait_ge(cent_ok, n + 1)
                a, q = amax_h[:, t:t + 1], qs_h[:, t:t + 1]
                link(v.tensor_reduce(a, hid[:, t, :], axis=AX_X, op=ALU.max, apply_absolute_value=True))
                link(v.reciprocal(q, a))
                link(ts(q, q, Q_B, None, ALU.mult))
                dve.wait_ge(hsq_ok, n + 1)
                ts(hid[:, t, :], hid[:, t, :], q, Q_B, ALU.mult, ALU.min).then_inc(hq_ok, 1)

            def split_hidden(b, t):
                for j in range(4):
                    k = 4 * (BT * b + t) + j + 1
                    dve.wait_ge(hqh_ok, k)
                    stt(hq_lo[:, t, 4 * j:4 * j + 4, :], HT[j][:, :].rearrange("p (a b) -> p a b", a=4), -Q_B,
                        hq_hi[:, t, 4 * j:4 * j + 4, :], ALU.max, ALU.subtract).then_inc(hql_ok, 1)

            def result_sum(b, s):
                product_scale(b, NH, sc_pr, amax_h, 1, scpr_ok)
                dve.wait_ge(scpr_ok, b + 1)
                for t in range(BT):
                    dve.wait_ge(pr_done, BT * b + t + 1)
                    if t == 0:
                        wait(dve, stored, 16 * b)
                    stt(y_out[:, t, :], PR[t][:, :], sc_pr[:, t:t + 1], x2[:, s, t, :], ALU.mult,
                        ALU.add).then_inc(pr_read, 1)
                dve.wait_ge(pr_read, BT * b + BT)
                norm_stats(NO, [y_out[:, t, :] for t in range(BT)], LN_EPS)

            def result_norm(b):
                for t in range(BT):
                    normalise(NO, b, t, y_out[:, t, :], y_out[:, t, :], out_ok)

            def row(b, s, first=False, final=False):
                r_stats(b)
                if not final:
                    input_sum(b + 1)
                second_norm(b, s)
                if not final:
                    input_norm(b + 1)
                quantise_x(b, s)
                if not final:
                    maxima(b + 1)
                split_x(b)
                product_scale(b, NQ, sc_fc, amax_x, 0, scfc_ok)
                if not first:
                    result_sum(b - 1, 1 - s)
                if not final:
                    states(b + 1)
                if not first:
                    result_norm(b - 1)
                if not final:
                    ratio(b + 1)
                for t in range(BT):
                    quantise_hidden(b, t)
                ts(var_e[:, NH, :], hssq[:, :], 1.0 / INNER, FFN_EPS, ALU.mult, ALU.add).then_inc(var_ok[NH], 1)
                for t in range(BT):
                    split_hidden(b, t)

            dve.wait_ge(decay_exp, HEADS + 1)
            ts(wneg[:, :], wneg[:, :], -1.0, None, ALU.mult).then_inc(w_ok, 1)
            ts(nfst[:, :], fst[:, :], -1.0, None, ALU.mult).then_inc(w_ok, 1)
            dve.wait_ge(w_ok, 2)
            dve.wait_ge(states0, 3)
            input_sum(0)
            input_norm(0)
            maxima(0)
            states(0)
            ratio(0)
            s0 = steps.n
            row(0, 0, first=True)
            s1 = steps.n
            row_steps = s1 - s0 + 6
            with dve.Fori(0, (BATCH - 2) // 2) as i:
                steps.base, steps.n = 2 * row_steps * i + s1, 0
                row(2 * i + 1, 1)
                assert steps.n == row_steps
                row(2 * i + 2, 0)
                assert steps.n == 2 * row_steps
            steps.base, steps.n = (BATCH - 2) * row_steps + s1, 0
            row(BATCH - 1, (BATCH - 1) % 2, final=True)
            result_sum(BATCH - 1, (BATCH - 1) % 2)
            result_norm(BATCH - 1)

        @block.gpsimd
        def _(pool):
            g_ = nc.gpsimd
            g_.memset(ident[:, :], 0.0).then_inc(pool_const, 1)
            g_.memset(ones[:, :], 1.0).then_inc(pool_const, 1)
            g_.memset(neg_half[:, :], -0.5).then_inc(pool_const, 1)
            g_.memset(sq_sum[:, :, :], 0.0).then_inc(pool_const, 1)
            g_.iota(dist_i, [[1, SEQ]], 0, -1).then_inc(dist_ok, 1)
            pool.wait_ge(dist_ok, 1)
            g_.tensor_scalar(dist, dist_i, 0.0, None, ALU.max).then_inc(dist_ok, 1)
            pool.wait_ge(pool_const, 4)
            g_.affine_select(out=ident[:, :], in_=ident[:, :], compare_op=ALU.not_equal, fill=1.0, base=0,
                             pattern=[[-1, P]], channel_multiplier=1).then_inc(ident_ok, 1)
            for h in range(HEADS):
                pool.wait_ge(decay_exp, h + 1)
                d = decays[:, h, 0:P]
                g_.affine_select(out=d, in_=d, compare_op=ALU.is_ge, fill=0.0, base=0, pattern=[[1, P]],
                                 channel_multiplier=-1).then_inc(decays_ok, 1)

            def clear(g):
                pool.wait_ge(x_lo_ok, g + 1)
                g_.memset(resid[:, 4 * g:4 * g + 4, :], 0.0).then_inc(x_zeroed, 1)

            def add_squares(u, g):
                pool.wait_ge(squared, u + 1)
                wait(pool, sq_added, u - GROUPS + 1)
                g_.tensor_tensor(sq_sum[:, g, :], sq_sum[:, g, :], o_sq[:, :], ALU.add).then_inc(sq_added, 1)

            clear(0)
            for g in range(1, GROUPS):
                clear(g)
                add_squares(g - 1, g - 1)
            add_squares(GROUPS - 1, GROUPS - 1)
            with pool.Fori(1, HEADS) as h:
                for g in range(GROUPS):
                    add_squares(GROUPS * h + g, g)
            pool.wait_ge(rms_in_ok, 1)
            g_.tensor_tensor(rms[:, :], rms_in[:, :], neg_half[:, :], ALU.pow).then_inc(rms_ok, 1)

            pool.wait_ge(rms_ok, 1)
            g_.memset(pp[:, :, 0:1], NEG_BIG).then_inc(states0, 1)
            g_.memset(aa[:, :, 0:1], 0.0).then_inc(states0, 1)
            g_.memset(bb[:, :, 0:1], 0.0).then_inc(states0, 1)
            pool.wait_ge(states0, 3)

            def root(k, b):
                pool.wait_ge(var_ok[k], b + 1)
                g_.tensor_tensor(rstd[:, k, :], var_e[:, k, :], neg_half[:, 0:BT], ALU.pow).then_inc(rstd_ok[k], 1)

            def differences(b):
                pool.wait_ge(pp_ok, KT * b + KT)
                g_.tensor_tensor(t1[:, :, :], pp[:, :, 0:SEQ], pp[:, :, 1:SQ], ALU.subtract).then_inc(t1d_ok, 1)
                g_.tensor_tensor(t2[:, :, :], key[:, :, :], pp[:, :, 0:SEQ], ALU.subtract).then_inc(kd_ok, 1)

            def inputs(b):
                pool.wait_ge(ctx_in, 16 * b + 16)
                pool.wait_ge(e2b_ok, b + 1)
                pool.wait_ge(e1b_ok, KT * b + KT)
                g_.tensor_tensor(t1[:, :, :], e2b[:, :, :], val[:, :, :], ALU.mult).then_inc(bv_ok, 1)
                pool.wait_ge(e_ok, 2 * b + 2)
                g_.tensor_tensor(t2[:, :, :], e2[:, :, :], val[:, :, :], ALU.mult).then_inc(ev_ok, 1)

            def fraction(b):
                wait(pool, r_turned, b)
                pool.wait_ge(scans_ok, 2 * KT * b + KT)
                g_.tensor_tensor(den[:, :, :], e1[:, :, :], bb[:, :, 0:SEQ], ALU.mult).then_inc(den1_ok, 1)
                pool.wait_ge(den1_ok, b + 1)
                g_.tensor_tensor(den[:, :, :], den[:, :, :], e2[:, :, :], ALU.add).then_inc(den_ok, 1)
                pool.wait_ge(scans_ok, 2 * KT * (b + 1))
                g_.tensor_tensor(num[:, :, :], e1[:, :, :], aa[:, :, 0:SEQ], ALU.mult).then_inc(num1_ok, 1)
                pool.wait_ge(num1_ok, b + 1)
                pool.wait_ge(ev_ok, b + 1)
                g_.tensor_tensor(num[:, :, :], num[:, :, :], t2[:, :, :], ALU.add).then_inc(num_ok, 1)

            def row(b, first=False, final=False):
                root(NR, b)
                if not final:
                    root(NX, b + 1)
                root(NQ, b)
                if not final:
                    differences(b + 1)
                    inputs(b + 1)
                if not first:
                    root(NO, b - 1)
                if not final:
                    fraction(b + 1)
                root(NH, b)

            root(NX, 0)
            differences(0)
            inputs(0)
            fraction(0)
            row(0, first=True)
            with pool.Fori(1, BATCH - 1) as b:
                row(b)
            row(BATCH - 1, final=True)
            root(NO, BATCH - 1)


def kernel(x, ctx_2048, L0_attn_slope_rate, L0_attn_Wqkv, L0_attn_Wg, L0_attn_norm_w, L0_attn_Wo,
           L0_xattn_time_decay, L0_xattn_time_first, L0_ffn_w_fc, L0_ffn_w_proj):
    import numpy as np
    import concourse.bacc as bacc
    from concourse.bass_utils import run_bass_kernel_spmd

    def tiled(w_t):
        return w_t.reshape(-1, P, w_t.shape[1]).transpose(1, 0, 2)

    x = np.asarray(x)
    x_t = tiled(x.reshape(TOKENS, HID).T).reshape(P, KT, GROUPS, GT).transpose(0, 2, 1, 3)
    x_rows = x.reshape(BATCH, BT, P, HID).transpose(0, 2, 1, 3)
    ctx_t = np.asarray(ctx_2048).reshape(BATCH, SEQ, KT, P).transpose(0, 3, 2, 1)
    qkv = np.asarray(L0_attn_Wqkv).reshape(HEADS, 3, DH, KT, P).transpose(0, 4, 1, 3, 2)
    gate = np.asarray(L0_attn_Wg).reshape(HEADS, 1, DH, KT, P).transpose(0, 4, 1, 3, 2)
    wo = np.asarray(L0_attn_Wo).T.reshape(HEADS, P, 1, HID)
    w_heads = np.concatenate([qkv.reshape(HEADS, P, 3, HID), gate.reshape(HEADS, P, 1, HID), wo], axis=2)
    slopes = np.broadcast_to(np.asarray(L0_attn_slope_rate).reshape(1, HEADS), (P, HEADS))
    norm_w = np.asarray(L0_attn_norm_w).reshape(HEADS, P).T
    decay = np.asarray(L0_xattn_time_decay).reshape(KT, P).T
    first = np.asarray(L0_xattn_time_first).reshape(KT, P).T
    w_ffn = np.concatenate([tiled(np.asarray(L0_ffn_w_fc).T).reshape(P, -1),
                            tiled(np.asarray(L0_ffn_w_proj).T).reshape(P, -1)], axis=1)
    w_ffn = w_ffn.reshape(P, CHUNKS, CW).transpose(1, 0, 2)
    laid = {"x_t": x_t, "x_rows": x_rows, "ctx_t": ctx_t, "w_heads": w_heads, "slopes": slopes,
            "norm_w": norm_w, "decay": decay, "first": first, "w_ffn": w_ffn}
    laid = {k: np.ascontiguousarray(a) for k, a in laid.items()}

    nc = bacc.Bacc("TRN2", target_bir_lowering=False, num_devices=1)
    args = {k: nc.dram_tensor(k, a.shape, F32, kind="ExternalInput").ap() for k, a in laid.items()}
    out = nc.dram_tensor("out", (BATCH, P, BT, HID), F32, kind="ExternalOutput").ap()
    decoder_layer(nc, **args, out=out)
    r = run_bass_kernel_spmd(nc, [laid], core_ids=[0])
    got = np.asarray(r.results[0]["out"])
    return got.transpose(0, 2, 1, 3).reshape(BATCH, SEQ, HID)
```

```python
from contextlib import ExitStack

import concourse.bass as bass
from concourse import mybir

P = 128
F32 = mybir.dt.float32
F32R = mybir.dt.float32r
F16 = mybir.dt.float16
ALU = mybir.AluOpType
ACT = mybir.ActivationFunctionType
AX_X = mybir.AxisListType.X

BATCH, SEQ, HID = 8, 256, 512
TOKENS = BATCH * SEQ
HEADS, DH = 16, 128
INNER = 2048
KT = HID // P
FT = INNER // P
GT = 512
GROUPS = TOKENS // GT
TILES = TOKENS // P
BT = SEQ // P
PROJ = 4
UNITS = HEADS * GROUPS
CHUNKS = 16
CW = KT * INNER * 2 // CHUNKS
LN_EPS = 1e-5
FFN_EPS = 1e-6
RMS_EPS = 1.1920928955078125e-07
Q_B = 128.0
NEG_BIG = -1e38
ABS_HEADS = 4
TERN_HEADS = 8
SQ = SEQ + 1


def decoder_layer(nc, x_t, x_rows, ctx_t, w_heads, slopes, norm_w, decay, first, w_ffn, out):
    with ExitStack() as ctx:
        def sem(name):
            return ctx.enter_context(nc.semaphore(name))

        def sb(name, shape, dt=F32, stack=ctx):
            return stack.enter_context(nc.sbuf_tensor(name, shape, dt))

        bank = [ctx.enter_context(nc.psum_tensor(f"bank{i}", [P, 512], F32)) for i in range(8)]

        resid = sb("resid", [P, TILES, HID])
        tern = sb("tern", [P, CHUNKS, CW], F16)
        ident = sb("ident", [P, P])
        ones = sb("ones", [P, P])
        neg_half = sb("neg_half", [P, TILES])
        neg_slope = sb("neg_slope", [P, HEADS])
        normw = sb("normw", [P, HEADS])
        dec = sb("dec", [P, KT])
        fst = sb("fst", [P, KT])
        slope_in = sb("slope_in", [P, HEADS])
        wneg = sb("wneg", [P, KT])
        abs_sum = sb("abs_sum", [P, CHUNKS])
        abs_two = sb("abs_two", [P, 2])
        thr = sb("thr", [P, 2, CHUNKS])
        wscale = sb("wscale", [P, 2])
        rms_in = sb("rms_in", [P, TILES])
        rms = sb("rms", [P, TILES])
        sq_sum = sb("sq_sum", [P, GROUPS, GT])
        nshift = sb("nshift", [P, 5, BT])
        stats = sb("stats", [P, 5, BT, 6])
        NORMS = NX, NR, NQ, NH, NO = range(5)
        mv = sb("mv", [P, len(NORMS), BT, 2])
        var_e = sb("var_e", [P, len(NORMS), BT])
        rstd = sb("rstd", [P, len(NORMS), BT])

        att = ExitStack()
        x_hi = sb("x_hi", [P, GROUPS, KT, GT], F32R, att)
        x_lo = sb("x_lo", [P, GROUPS, KT, GT], F32R, att)
        raw = sb("raw", [P, PROJ, HID], F32, att)
        w_hi = sb("w_hi", [P, PROJ, KT, DH], F32R, att)
        w_lo = sb("w_lo", [P, PROJ, KT, DH], F32R, att)
        wo_hi = sb("wo_hi", [P, HID], F32R, att)
        wo_lo = sb("wo_lo", [P, HID], F32R, att)
        decays = sb("decays", [P, 2, SEQ], F32, att)
        tri = sb("tri", [P, P], F32, att)
        dist = sb("dist", [P, SEQ], F32, att)
        q_t = sb("q_t", [P, GT], F32, att)
        k_t = sb("k_t", [P, GT], F32, att)
        v_t = sb("v_t", [P, GT], F32, att)
        v_r = sb("v_r", [P, KT, P], F32, att)
        g_t = sb("g_t", [P, GT], F32, att)
        probs = sb("probs", [P, 2, 3 * P], F32, att)
        q_hi = sb("q_hi", [P, GT], F32R, att)
        q_lo = sb("q_lo", [P, GT], F32R, att)
        k_hi = sb("k_hi", [P, 2, P], F32R, att)
        k_lo = sb("k_lo", [P, 2, P], F32R, att)
        v_hi = sb("v_hi", [P, 2, P], F32R, att)
        v_lo = sb("v_lo", [P, 2, P], F32R, att)
        p_hi = sb("p_hi", [P, 2, SEQ], F32R, att)
        p_lo = sb("p_lo", [P, 2, SEQ], F32R, att)
        gated = sb("gated", [P, GT], F32, att)
        u_hi = sb("u_hi", [P, GT], F32R, att)
        u_lo = sb("u_lo", [P, GT], F32R, att)
        o_sq = sb("o_sq", [P, GT], F32, att)
        w_raw = sb("w_raw", [P, CW], F32, att)
        dist_i = o_sq[:, 0:SEQ].bitcast(mybir.dt.int32)
        att.close()

        ffn = ExitStack()
        x_in = sb("x_in", [P, BT, HID], F32, ffn)
        x1 = sb("x1", [P, BT, HID], F32, ffn)
        val = sb("val", [P, KT, SEQ], F32, ffn)
        key = sb("key", [P, KT, SEQ], F32, ffn)
        pp = sb("pp", [P, KT, SQ], F32, ffn)
        aa = sb("aa", [P, KT, SQ], F32, ffn)
        bb = sb("bb", [P, KT, SQ], F32, ffn)
        e1b = sb("e1b", [P, KT, SEQ], F32, ffn)
        e2b = sb("e2b", [P, KT, SEQ], F32, ffn)
        e1 = sb("e1", [P, KT, SEQ], F32, ffn)
        e2 = sb("e2", [P, KT, SEQ], F32, ffn)
        t1 = sb("t1", [P, KT, SEQ], F32, ffn)
        t2 = sb("t2", [P, KT, SEQ], F32, ffn)
        num = sb("num", [P, KT, SEQ], F32, ffn)
        den = sb("den", [P, KT, SEQ], F32, ffn)
        x2 = sb("x2", [P, 2, BT, HID], F32, ffn)
        xq = sb("xq", [P, BT, HID], F32, ffn)
        xq_hi = sb("xq_hi", [P, BT, KT, P], F16, ffn)
        xq_lo = sb("xq_lo", [P, BT, KT, P], F16, ffn)
        hid = sb("hid", [P, BT, INNER], F32, ffn)
        hid_sq = sb("hid_sq", [P, INNER], F32, ffn)
        hq_hi = sb("hq_hi", [P, BT, FT, P], F16, ffn)
        hq_lo = sb("hq_lo", [P, BT, FT, P], F16, ffn)
        y_out = sb("y_out", [P, BT, HID], F32, ffn)
        amax_x = sb("amax_x", [P, BT], F32, ffn)
        amax_h = sb("amax_h", [P, BT], F32, ffn)
        qs_x = sb("qs_x", [P, BT], F32, ffn)
        qs_h = sb("qs_h", [P, BT], F32, ffn)
        sc_fc = sb("sc_fc", [P, BT], F32, ffn)
        sc_pr = sb("sc_pr", [P, BT], F32, ffn)
        hsum = sb("hsum", [P, BT, 4], F32, ffn)
        hsum_dump = sb("hsum_dump", [P, 4], F32, ffn)
        nmean = sb("nmean", [P, BT], F32, ffn)
        hssq = sb("hssq", [P, BT], F32, ffn)
        ffn.close()

        slopes_in, small_in = sem("slopes_in"), sem("small_in")
        xraw_in = [sem(f"xraw_in{i}") for i in range(KT + GROUPS - 1)]
        wq_in, wraw_in, woraw_in = sem("wq_in"), sem("wraw_in"), sem("woraw_in")
        fraw_in = sem("fraw_in")
        x_hi_ok, x_lo_ok, x_zeroed = sem("x_hi_ok"), sem("x_lo_ok"), sem("x_zeroed")
        wsplit_hi, wsplit = sem("wsplit_hi"), sem("wsplit")
        wo_scaled, wo_hi_ok, wo_split = sem("wo_scaled"), sem("wo_hi_ok"), sem("wo_split")
        pool_const, dist_ok, dve_const = sem("pool_const"), sem("dist_ok"), sem("dve_const")
        decay_exp, decays_ok, ident_ok = sem("decay_exp"), sem("decays_ok"), sem("ident_ok")
        tri_ok = sem("tri_ok")
        projected, evacuated = sem("projected"), sem("evacuated")
        scored, masked_off, masked = sem("scored"), sem("masked_off"), sem("masked")
        v_turned, v_ready = sem("v_turned"), sem("v_ready")
        q_hi_ok, k_hi_ok, q_split, k_split = sem("q_hi_ok"), sem("k_hi_ok"), sem("q_split"), sem("k_split")
        v_hi_ok, v_split, p_hi_ok, p_split = sem("v_hi_ok"), sem("v_split"), sem("p_hi_ok"), sem("p_split")
        mixed, squared, sq_added = sem("mixed"), sem("squared"), sem("sq_added")
        gate_done, u_hi_ok, u_ok = sem("gate_done"), sem("u_hi_ok"), sem("u_ok")
        y_done, y_added = sem("y_done"), sem("y_added")
        abs_ok, abs_two_ok, gamma_ok = sem("abs_ok"), sem("abs_two_ok"), sem("gamma_ok")
        thr_ok, picked, terned = sem("thr_ok"), sem("picked"), sem("terned")
        sq_total, rms_in_ok, rms_ok = sem("sq_total"), sem("rms_in_ok"), sem("rms_ok")
        xin_in, ctx_in = sem("xin_in"), sem("ctx_in")
        wneg_exp, w_ok, states0 = sem("wneg_exp"), sem("w_ok"), sem("states0")
        dstep = sem("dstep")
        var_ok = [sem(f"var_ok{k}") for k in NORMS]
        rstd_ok = [sem(f"rstd_ok{k}") for k in NORMS]
        x1_ok, x1_turned, key_ok = sem("x1_ok"), sem("x1_turned"), sem("key_ok")
        pp_ok, t1d_ok, kd_ok, e1b_ok, e2d_ok = sem("pp_ok"), sem("t1d_ok"), sem("kd_ok"), sem("e1b_ok"), sem("e2d_ok")
        bounds_ok, e1_ok, e2_ok, e2b_ok, bv_ok = sem("bounds_ok"), sem("e1_ok"), sem("e2_ok"), sem("e2b_ok"), sem("bv_ok")
        ev_ok, den1_ok, den_ok = sem("ev_ok"), sem("den1_ok"), sem("den_ok")
        num1_ok, num_ok = sem("num1_ok"), sem("num_ok")
        inv_ok, y_ok = sem("inv_ok"), sem("y_ok")
        scans_ok, r_ok, r_turned, x2_ok = sem("scans_ok"), sem("r_ok"), sem("r_turned"), sem("x2_ok")
        xq_ok, xq_turned, xqh_ok, xql_ok = sem("xq_ok"), sem("xq_turned"), sem("xqh_ok"), sem("xql_ok")
        fc_done, gelu_ok, mean_ok, cent_ok = sem("fc_done"), sem("gelu_ok"), sem("mean_ok"), sem("cent_ok")
        hsq_ok, scpr_ok = sem("hsq_ok"), sem("scpr_ok")
        shift_ok = [sem(f"shift_ok{k}") for k in NORMS]
        hq_ok, hq_turned, hqh_ok, hql_ok = sem("hq_ok"), sem("hq_turned"), sem("hqh_ok"), sem("hql_ok")
        pr_done, pr_read, scfc_ok, out_ok, stored = sem("pr_done"), sem("pr_read"), sem("scfc_ok"), sem("out_ok"), sem("stored")

        PJ = bank[0:2]
        SC = bank[2:4]
        OT, VT = bank[4], bank[5]
        YB = bank[6:8]
        Q, K, V, G = range(PROJ)

        TR = bank[0:2]
        FC = bank[3:5] + bank[0:2]
        QT = bank[5:7]
        HT = bank[3:7]
        PR = [bank[7], bank[2]]

        block = ctx.enter_context(nc.Block())

        def first_keys(t):
            return t[:, :].rearrange("p (b j) -> p b j", b=2)[:, :, 0:P]

        def wait(eng, s, value):
            if not isinstance(value, int) or value > 0:
                eng.wait_ge(s, value)

        @block.sync
        def _(sp):
            sp.dma_start(slope_in[:, :], slopes).then_inc(slopes_in, 16)
            sp.dma_start(raw[:, Q, :], w_heads[0, :, Q, :]).then_inc(wq_in, 16)
            for kt in range(KT):
                sp.dma_start(resid[:, kt, :], x_t[:, 0, kt, :]).then_inc(xraw_in[kt], 16)
            sp.dma_start(raw[:, K:PROJ, :], w_heads[0, :, K:PROJ, :]).then_inc(wraw_in, 16)
            sp.dma_start(resid[:, 4:8, :], x_t[:, 1, :, :]).then_inc(xraw_in[KT], 16)
            for dst, src in ((normw, norm_w), (dec, decay), (fst, first)):
                sp.dma_start(dst[:, :], src).then_inc(small_in, 16)
            sp.wait_ge(wsplit, 1)
            sp.dma_start(raw[:, 0, :], w_heads[0, :, PROJ, :]).then_inc(woraw_in, 16)
            for g in range(2, GROUPS):
                sp.dma_start(resid[:, 4 * g:4 * g + 4, :], x_t[:, g, :, :]).then_inc(xraw_in[KT + g - 1], 16)
            sp.wait_ge(wsplit, PROJ)
            sp.wait_ge(wo_split, 1)
            sp.dma_start(raw[:, :, :], w_heads[1, :, 0:PROJ, :]).then_inc(wraw_in, 16)
            sp.dma_start(w_raw[:, :], w_ffn[0, :, :]).then_inc(fraw_in, 16)

            def load_wo(h):
                sp.wait_ge(wsplit, PROJ * h + 1)
                sp.dma_start(raw[:, 0, :], w_heads[h, :, PROJ, :]).then_inc(woraw_in, 16)

            def load_next_head(h, after):
                sp.wait_ge(wo_split, h + 1)
                sp.dma_start(raw[:, :, :], w_heads[after, :, 0:PROJ, :]).then_inc(wraw_in, 16)

            def load_ffn(read, count, chunk):
                sp.wait_ge(read, count)
                sp.dma_start(w_raw[:, :], w_ffn[chunk, :, :]).then_inc(fraw_in, 16)

            def load_head_a(h, after, chunks):
                load_wo(h)
                load_ffn(abs_ok, 4 * h - 3, chunks[0])
                load_next_head(h, after)
                for i in range(1, 4):
                    load_ffn(abs_ok, 4 * h - 3 + i, chunks[i])

            with sp.Fori(1, ABS_HEADS) as h:
                after = sp.snap(h + 1)
                load_head_a(h, after, [sp.snap(4 * h - 3 + i) for i in range(4)])
            load_head_a(ABS_HEADS, ABS_HEADS + 1, [CHUNKS - 3, CHUNKS - 2, CHUNKS - 1, 0])
            h0 = ABS_HEADS + 1
            with sp.Fori(h0, h0 + TERN_HEADS - 1) as h:
                after, chunk, chunk1 = sp.snap(h + 1), sp.snap(2 * h - 2 * h0 + 1), sp.snap(2 * h - 2 * h0 + 2)
                load_wo(h)
                load_ffn(terned, 2 * h - 2 * h0 + 1, chunk)
                load_next_head(h, after)
                load_ffn(terned, 2 * h - 2 * h0 + 2, chunk1)
            for h in range(h0 + TERN_HEADS - 1, HEADS):
                load_wo(h)
                if h == h0 + TERN_HEADS - 1:
                    load_ffn(terned, CHUNKS - 1, CHUNKS - 1)
                if h < HEADS - 1:
                    load_next_head(h, h + 1)

            def load_rows(b):
                wait(sp, x1_ok, BT * b)
                sp.dma_start(x_in[:, :, :], x_rows[b, :, :, :]).then_inc(xin_in, 16)

            def load_ctx(b):
                wait(sp, ev_ok, b)
                sp.dma_start(val[:, :, :], ctx_t[b, :, :, :]).then_inc(ctx_in, 16)

            def store(b):
                sp.wait_ge(out_ok, BT * b + BT)
                sp.dma_start(out[b, :, :, :], y_out[:, :, :]).then_inc(stored, 16)

            sp.wait_ge(projected, PROJ * (UNITS - 3))
            load_rows(0)
            sp.wait_ge(projected, PROJ * (UNITS - 2))
            load_ctx(0)
            load_rows(1)
            load_ctx(1)
            load_rows(2)
            with sp.Fori(1, BATCH - 2) as b:
                ctx_row, x_row, row_out = sp.snap(b + 1), sp.snap(b + 2), sp.snap(b - 1)
                load_ctx(ctx_row)
                load_rows(x_row)
                store(row_out)
            load_ctx(BATCH - 1)
            for b in range(BATCH - 3, BATCH):
                store(b)
            sp.wait_ge(stored, 16 * BATCH)

        @block.tensor
        def _(pe):
            mm = nc.tensor.matmul

            def project(h, g, j, fresh=False):
                n = PROJ * (GROUPS * h + g) + j
                if g == 0:
                    pe.wait_ge(wsplit, PROJ * h + j + 1)
                wait(pe, evacuated, n - 1)
                for kt in range(KT):
                    if fresh:
                        pe.wait_ge(x_lo_ok, KT * g + kt + 1)
                    a, b = w_hi[:, j, kt, :], w_lo[:, j, kt, :]
                    c, d = x_hi[:, g, kt, :], x_lo[:, g, kt, :]
                    mm(PJ[j % 2][:, :], a, c, start=kt == 0, stop=False)
                    mm(PJ[j % 2][:, :], a, d, start=False, stop=False)
                    last = mm(PJ[j % 2][:, :], b, c, start=False, stop=kt == KT - 1)
                last.then_inc(projected, 1)

            def scores(u, b):
                pe.wait_ge(q_split, u + 1)
                pe.wait_ge(k_split, u + 1)
                wait(pe, masked, 2 * u + b - 1)
                o = b * SEQ
                wide = SC[b][:, 0:SEQ]
                mm(wide, k_hi[:, b, :], q_hi[:, o:o + SEQ], start=True, stop=False)
                mm(wide, k_hi[:, b, :], q_lo[:, o:o + SEQ], start=False, stop=False)
                mm(wide, k_lo[:, b, :], q_hi[:, o:o + SEQ], start=False, stop=True)
                mm(SC[b][:, SEQ:SEQ + P], k_t[:, o + P:o + SEQ], q_t[:, o + P:o + SEQ],
                   start=True, stop=True).then_inc(scored, 1)

            def mix(u):
                pe.wait_ge(v_ready, u + 1)
                pe.wait_ge(v_split, u + 1)
                wait(pe, squared, u)
                for b in range(2):
                    pe.wait_ge(masked, 2 * u + b + 1)
                    pe.wait_ge(p_split, 2 * u + b + 1)
                    o = b * SEQ
                    wide = OT[:, o:o + SEQ]
                    mm(wide, v_hi[:, b, :], p_hi[:, b, :], start=True, stop=False)
                    mm(wide, v_hi[:, b, :], p_lo[:, b, :], start=False, stop=False)
                    mm(wide, v_lo[:, b, :], p_hi[:, b, :], start=False, stop=False)
                    last = mm(OT[:, o + P:o + SEQ], v_r[:, 2 * b + 1, :], probs[:, b, SEQ:SEQ + P],
                              start=False, stop=True)
                last.then_inc(mixed, 1)

            def turn_v(u):
                pe.wait_ge(evacuated, PROJ * u + V + 1)
                wait(pe, v_ready, u)
                for t in range(KT):
                    last = nc.tensor.transpose(VT[:, t * P:(t + 1) * P], v_t[:, t * P:(t + 1) * P], ident[:, :])
                last.then_inc(v_turned, 1)

            def output(h, u, tt):
                if tt == 0:
                    pe.wait_ge(u_ok, u + 1)
                    pe.wait_ge(wo_split, h + 1)
                wait(pe, y_added, 4 * u + tt - 1)
                c = slice(tt * P, (tt + 1) * P)
                mm(YB[tt % 2][:, :], u_hi[:, c], wo_hi[:, :], start=True, stop=False)
                mm(YB[tt % 2][:, :], u_hi[:, c], wo_lo[:, :], start=False, stop=False)
                mm(YB[tt % 2][:, :], u_lo[:, c], wo_hi[:, :], start=False, stop=True).then_inc(y_done, 1)

            def square_totals(g0, g1):
                for t in range(KT * g0, KT * g1):
                    last = mm(VT[:, t:t + 1], sq_sum[:, t // 4, (t % 4) * P:(t % 4 + 1) * P], ones[:, 0:1],
                              start=True, stop=True)
                last.then_inc(sq_total, 1)

            def unit(h, g, lag1=True, lag2=True, fresh=False, final=False):
                u = GROUPS * h + g
                before2 = h if g >= 2 else h - 1
                if lag1:
                    scores(u - 1, 0)
                    scores(u - 1, 1)
                if final:
                    pe.wait_ge(sq_added, UNITS - 3)
                    pe.wait_ge(v_ready, UNITS - 1)
                    square_totals(0, 1)
                project(h, g, Q, fresh)
                if lag2:
                    output(before2, u - 2, 0)
                    output(before2, u - 2, 1)
                project(h, g, K)
                if lag2:
                    output(before2, u - 2, 2)
                    output(before2, u - 2, 3)
                project(h, g, V)
                if lag1:
                    mix(u - 1)
                project(h, g, G)
                if final:
                    pe.wait_ge(rms_in_ok, 1)
                turn_v(u)

            pe.wait_ge(ident_ok, 1)
            for g in range(GROUPS):
                unit(0, g, g >= 1, g >= 2, fresh=True)
            with pe.Fori(1, ABS_HEADS + 1) as h:
                for g in range(GROUPS):
                    unit(h, g)
            pe.wait_ge(abs_two_ok, 1)
            pe.wait_ge(masked, 2 * (GROUPS * (ABS_HEADS + 1) - 1))
            mm(SC[0][:, 0:2], ones[:, :], abs_two[:, :], start=True, stop=True).then_inc(gamma_ok, 1)
            pe.wait_ge(thr_ok, 3)
            with pe.Fori(ABS_HEADS + 1, HEADS - 1) as h:
                for g in range(GROUPS):
                    unit(h, g)
            for g in range(GROUPS):
                unit(HEADS - 1, g, final=g == GROUPS - 1)
            def turn_x1(b):
                pe.wait_ge(x1_ok, BT * b + BT)
                wait(pe, x2_ok, BT * b)
                for ct in range(KT):
                    for t in range(BT):
                        o = (ct % 2) * SEQ + t * P
                        last = nc.tensor.transpose(TR[ct // 2][:, o:o + P], x1[:, t, ct * P:(ct + 1) * P],
                                                   ident[:, :])
                last.then_inc(x1_turned, 1)

            def turn_back(b):
                pe.wait_ge(r_ok, b + 1)
                wait(pe, gelu_ok, 4 * BT * b)
                pe.wait_ge(key_ok, 2 * b + 2)
                for t in range(BT):
                    for ct in range(KT):
                        last = nc.tensor.transpose(TR[t][:, ct * P:(ct + 1) * P], num[:, ct, t * P:(t + 1) * P],
                                                   ident[:, :])
                last.then_inc(r_turned, 1)

            def turn_xq(b, t):
                pe.wait_ge(xq_ok, BT * b + t + 1)
                wait(pe, hql_ok, 4 * BT * b)
                for kt in range(KT):
                    last = nc.tensor.transpose(QT[t][:, kt * P:(kt + 1) * P], xq[:, t, kt * P:(kt + 1) * P],
                                               ident[:, :])
                last.then_inc(xq_turned, 1)

            def fc(b, t, final=False):
                n = BT * b + t
                pe.wait_ge(xqh_ok, n + 1)
                pe.wait_ge(xql_ok, n + 1)
                for f in range(4):
                    wait(pe, gelu_ok, 4 * n + f - 3)
                    if t == 0 and f == 2 and not final:
                        pe.wait_ge(key_ok, 2 * b + 4)
                    for kt in range(KT):
                        c = kt * INNER + f * 512
                        w = tern[:, c // CW, c % CW:c % CW + 512]
                        mm(FC[f][:, :], xq_hi[:, t, kt, :], w, start=kt == 0, stop=False)
                        last = mm(FC[f][:, :], xq_lo[:, t, kt, :], w, start=False, stop=kt == KT - 1)
                    last.then_inc(fc_done, 1)

            def turn_hq(b, t):
                n = BT * b + t
                pe.wait_ge(gelu_ok, 4 * BT * (b + 1))
                pe.wait_ge(hq_ok, n + 1)
                for j in range(4):
                    if t > 0:
                        pe.wait_ge(hql_ok, 4 * (n - 1) + j + 1)
                    for i in range(4):
                        k = 4 * j + i
                        last = nc.tensor.transpose(HT[j][:, i * P:(i + 1) * P], hid[:, t, k * P:(k + 1) * P],
                                                   ident[:, :])
                    last.then_inc(hq_turned, 1)

            def proj(b, t, k0=0, k1=FT):
                n = BT * b + t
                if k0 == 0:
                    pe.wait_ge(hqh_ok, 4 * n + 4)
                    pe.wait_ge(hql_ok, 4 * n + 4)
                    wait(pe, pr_read, n - 1)
                for k in range(k0, k1):
                    c = KT * INNER + k * HID
                    w = tern[:, c // CW, c % CW:c % CW + HID]
                    mm(PR[t][:, :], hq_hi[:, t, k, :], w, start=k == 0, stop=False)
                    last = mm(PR[t][:, :], hq_lo[:, t, k, :], w, start=False, stop=k == FT - 1)
                if k1 == FT:
                    last.then_inc(pr_done, 1)

            K_A, K_B = 6, 12

            def row(b, first=False, final=False):
                if not first:
                    proj(b - 1, 1, 0, K_A)
                if not final:
                    turn_x1(b + 1)
                if not first:
                    proj(b - 1, 1, K_A, K_B)
                for t in range(BT):
                    turn_xq(b, t)
                if not first:
                    proj(b - 1, 1, K_B, FT)
                for t in range(BT):
                    fc(b, t, final)
                if final:
                    turn_hq(b, 0)
                    proj(b, 0, 0, K_B)
                    turn_hq(b, 1)
                    proj(b, 0, K_B, FT)
                    proj(b, 1)
                else:
                    turn_hq(b, 0)
                    turn_back(b + 1)
                    turn_hq(b, 1)
                    proj(b, 0)

            U = UNITS
            scores(U - 1, 0)
            scores(U - 1, 1)
            pe.wait_ge(evacuated, PROJ * U)
            turn_x1(0)
            for tt in range(4):
                output(HEADS - 1, U - 2, tt)
            mix(U - 1)
            for tt in range(4):
                output(HEADS - 1, U - 1, tt)
            pe.wait_ge(sq_added, U)
            pe.wait_ge(v_ready, U)
            square_totals(1, GROUPS)
            turn_back(0)
            pe.wait_ge(terned, CHUNKS)
            pe.wait_ge(rms_in_ok, 2)
            pe.wait_ge(y_added, 4 * U)
            row(0, first=True)
            with pe.Fori(1, BATCH - 1) as b:
                row(b)
            row(BATCH - 1, final=True)

        @block.scalar
        def _(act):
            fn = nc.scalar.activation

            def decay(h):
                wait(act, masked, 2 * GROUPS * (h - 1))
                fn(decays[:, bass.ds(h & 1, 1), :], dist[:, :], ACT.Exp,
                   scale=neg_slope[:, bass.ds(h, 1)]).then_inc(decay_exp, 1)

            def split_x(g, kt):
                act.wait_ge(xraw_in[kt] if g == 0 else xraw_in[KT + g - 1], 16)
                fn(x_hi[:, g, kt, :], resid[:, 4 * g + kt, :], ACT.Copy).then_inc(x_hi_ok, 1)

            def evacuate(u, j):
                act.wait_ge(projected, PROJ * u + j + 1)
                if j in (Q, K):
                    wait(act, scored, 2 * u)
                    dst = (q_t, k_t)[j][:, :]
                elif j == V:
                    wait(act, v_turned, u)
                    dst = v_t[:, :]
                else:
                    wait(act, gate_done, u)
                    dst = g_t[:, :]
                src = PJ[j % 2][:, :]
                if j == G:
                    fn(dst, src, ACT.Tanh, scale=0.5).then_inc(evacuated, 1)
                else:
                    fn(dst, src, ACT.Silu).then_inc(evacuated, 1)

            def square(u):
                act.wait_ge(gate_done, u + 1)
                wait(act, sq_added, u)
                fn(o_sq[:, :], OT[:, :], ACT.Square).then_inc(squared, 1)

            def split_q(u):
                act.wait_ge(evacuated, PROJ * u + Q + 1)
                fn(q_hi[:, :], q_t[:, :], ACT.Copy).then_inc(q_hi_ok, 1)

            def split_k(u):
                act.wait_ge(evacuated, PROJ * u + K + 1)
                fn(k_hi[:, :, :], first_keys(k_t), ACT.Copy).then_inc(k_hi_ok, 1)

            def split_probs(u):
                for b in range(2):
                    act.wait_ge(masked_off, 2 * u + b + 1)
                    fn(p_hi[:, b, :], probs[:, b, 0:SEQ], ACT.Copy).then_inc(p_hi_ok, 1)

            def copy_v(u):
                act.wait_ge(v_turned, u + 1)
                wait(act, mixed, u)
                fn(v_hi[:, :, :], first_keys(VT), ACT.Copy).then_inc(v_hi_ok, 1)
                fn(v_r[:, :, :], VT[:, :].rearrange("p (a b) -> p a b", a=KT), ACT.Copy).then_inc(v_ready, 1)

            def unit(h, g, lag1=True, split=None):
                u = GROUPS * h + g
                for j in (Q, K, V):
                    evacuate(u, j)
                    if j == Q:
                        split_q(u)
                        if lag1:
                            split_probs(u - 1)
                    if j == K:
                        split_k(u)
                    if j == K and split:
                        for kt in range(KT):
                            split_x(split, kt)
                if lag1:
                    square(u - 1)
                evacuate(u, G)
                copy_v(u)

            act.wait_ge(dist_ok, 2)
            act.wait_ge(dve_const, 1)
            decay(0)
            for kt in range(KT):
                split_x(0, kt)
            for g in range(GROUPS):
                unit(0, g, g >= 1, split=g + 1 if g < GROUPS - 1 else None)
                if g == 1:
                    decay(1)
                    act.wait_ge(small_in, 16 * 3)
                    fn(wneg[:, :], dec[:, :], ACT.Exp).then_inc(wneg_exp, 1)
            with act.Fori(1, HEADS - 1) as h:
                for g in range(GROUPS):
                    unit(h, g)
                    if g == 1:
                        decay(h + 1)
            for g in range(GROUPS):
                unit(HEADS - 1, g)
            def copy_key(b):
                act.wait_ge(x1_turned, b + 1)
                wait(act, r_ok, b)
                for c in range(2):
                    fn(key[:, 2 * c:2 * c + 2, :], TR[c][:, :].rearrange("p (a b) -> p a b", a=2),
                       ACT.Copy).then_inc(key_ok, 1)

            def exps(b):
                act.wait_ge(t1d_ok, b + 1)
                for c in range(KT):
                    fn(e1b[:, c, :], t1[:, c, :], ACT.Exp, bias=wneg[:, c:c + 1]).then_inc(e1b_ok, 1)
                act.wait_ge(e2d_ok, b + 1)
                fn(e2b[:, :, :], e2b[:, :, :], ACT.Exp).then_inc(e2b_ok, 1)
                act.wait_ge(bounds_ok, 2 * KT * (b + 1))
                fn(e1[:, :, :], e1[:, :, :], ACT.Exp, scale=-1.0).then_inc(e1_ok, 1)
                fn(e2[:, :, :], e2[:, :, :], ACT.Exp).then_inc(e2_ok, 1)

            def split_xq(b, t):
                act.wait_ge(xq_turned, BT * b + t + 1)
                fn(xq_hi[:, t, :, :], QT[t][:, :].rearrange("p (a b) -> p a b", a=KT), ACT.Copy).then_inc(xqh_ok, 1)

            def gelu(b, t, f):
                n = BT * b + t
                if f == 0:
                    wait(act, hq_turned, 4 * (n - 1))
                act.wait_ge(fc_done, 4 * n + f + 1)
                fn(hid[:, t, f * 512:(f + 1) * 512], FC[f][:, :], ACT.Gelu, scale=sc_fc[:, t:t + 1],
                   accum_out=hsum[:, t, f:f + 1]).then_inc(gelu_ok, 1)

            def centre(b, t):
                n = BT * b + t
                act.wait_ge(gelu_ok, 4 * n + 4)
                fn(hsum_dump[:, :], hsum[:, t, :], ACT.Identity, scale=-1.0 / INNER,
                   accum_out=nmean[:, t:t + 1]).then_inc(mean_ok, 1)
                act.wait_ge(mean_ok, n + 1)
                fn(hid[:, t, :], hid[:, t, :], ACT.Identity, bias=nmean[:, t:t + 1]).then_inc(cent_ok, 1)

            def variance(b, t):
                n = BT * b + t
                act.wait_ge(cent_ok, n + 1)
                fn(hid_sq[:, :], hid[:, t, :], ACT.Square, accum_out=hssq[:, t:t + 1]).then_inc(hsq_ok, 1)

            def result_norm(b):
                act.wait_ge(shift_ok[NO], b + 1)
                for t in range(BT):
                    fn(y_out[:, t, :], y_out[:, t, :], ACT.Identity, scale=rstd[:, NO, t:t + 1],
                       bias=nshift[:, NO, t:t + 1]).then_inc(out_ok, 1)

            def first_norms(b, final):
                act.wait_ge(shift_ok[NR], b + 1)
                for t in range(BT):
                    fn(x2[:, bass.ds(b & 1, 1), t, :], TR[t][:, :], ACT.Identity, scale=rstd[:, NR, t:t + 1],
                       bias=nshift[:, NR, t:t + 1]).then_inc(x2_ok, 1)
                if not final:
                    act.wait_ge(shift_ok[NX], b + 1)
                    for t in range(BT):
                        fn(x1[:, t, :], x1[:, t, :], ACT.Identity, scale=rstd[:, NX, t:t + 1],
                           bias=nshift[:, NX, t:t + 1]).then_inc(x1_ok, 1)

            def split_hq(b, t):
                n = BT * b + t
                wait(act, pr_done, n - 1)
                for j in range(4):
                    act.wait_ge(hq_turned, 4 * n + j + 1)
                    fn(hq_hi[:, t, 4 * j:4 * j + 4, :], HT[j][:, :].rearrange("p (a b) -> p a b", a=4),
                       ACT.Copy).then_inc(hqh_ok, 1)

            def row(b, first=False, final=False):
                first_norms(b, final)
                if not final:
                    copy_key(b + 1)
                for t in range(BT):
                    split_xq(b, t)
                if not final:
                    exps(b + 1)
                act.wait_ge(scfc_ok, b + 1)
                for f in range(4):
                    gelu(b, 0, f)
                centre(b, 0)
                gelu(b, 1, 0)
                gelu(b, 1, 1)
                variance(b, 0)
                gelu(b, 1, 2)
                gelu(b, 1, 3)
                if final:
                    split_hq(b, 0)
                centre(b, 1)
                if final:
                    variance(b, 1)
                    result_norm(b - 1)
                    split_hq(b, 1)
                else:
                    variance(b, 1)
                    for t in range(BT):
                        split_hq(b, t)
                    if not first:
                        result_norm(b - 1)

            split_probs(UNITS - 1)
            act.wait_ge(w_ok, 1)
            copy_key(0)
            exps(0)
            square(UNITS - 1)
            row(0, first=True)
            with act.Fori(1, BATCH - 1) as b:
                row(b)
            row(BATCH - 1, final=True)
            result_norm(BATCH - 1)

        @block.vector
        def _(dve):
            v = nc.vector
            stt, tt, ts = v.scalar_tensor_tensor, v.tensor_tensor, v.tensor_scalar

            def split_w(h, j):
                if isinstance(h, int) and h == 0 and j == Q:
                    dve.wait_ge(wq_in, 16)
                else:
                    dve.wait_ge(wraw_in, 16 * h + 16)
                wait(dve, projected, PROJ * (GROUPS * h - 1) + j + 1)
                k = PROJ * h + j + 1
                v.tensor_copy(w_hi[:, j, :, :], raw[:, j, :].rearrange("p (a b) -> p a b", a=KT)).then_inc(wsplit_hi, 1)
                dve.wait_ge(wsplit_hi, k)
                tt(w_lo[:, j, :, :], raw[:, j, :].rearrange("p (a b) -> p a b", a=KT),
                   w_hi[:, j, :, :].bitcast(F32), ALU.subtract).then_inc(wsplit, 1)

            def split_wo(h):
                dve.wait_ge(woraw_in, 16 * h + 16)
                wait(dve, y_done, 4 * GROUPS * h)
                ts(raw[:, 0, :], raw[:, 0, :], normw[:, bass.ds(h, 1)], 0.5, ALU.mult, ALU.mult).then_inc(wo_scaled, 1)
                dve.wait_ge(wo_scaled, h + 1)
                v.tensor_copy(wo_hi[:, :], raw[:, 0, :]).then_inc(wo_hi_ok, 1)
                dve.wait_ge(wo_hi_ok, h + 1)
                tt(wo_lo[:, :], raw[:, 0, :], wo_hi[:, :].bitcast(F32), ALU.subtract).then_inc(wo_split, 1)

            def mask(h, u, b):
                dve.wait_ge(scored, 2 * u + b + 1)
                wait(dve, mixed, u)
                hh = bass.ds(h & 1, 1)
                tt(probs[:, b, 0:SEQ], SC[b][:, 0:SEQ], decays[:, hh, :], ALU.mult).then_inc(masked_off, 1)
                tt(probs[:, b, SEQ:SEQ + P], SC[b][:, SEQ:SEQ + P], decays[:, hh, 0:P], ALU.mult).then_inc(masked, 1)

            def split_q(u):
                dve.wait_ge(q_hi_ok, u + 1)
                wait(dve, scored, 2 * u)
                tt(q_lo[:, :], q_t[:, :], q_hi[:, :].bitcast(F32), ALU.subtract).then_inc(q_split, 1)

            def split_k(u):
                dve.wait_ge(k_hi_ok, u + 1)
                tt(k_lo[:, :, :], first_keys(k_t), k_hi[:, :, :].bitcast(F32), ALU.subtract).then_inc(k_split, 1)

            def split_v(u):
                dve.wait_ge(v_ready, u + 1)
                tt(v_lo[:, :, :], v_r[:, :, :].rearrange("p (b j) f -> p b j f", b=2)[:, :, 0, :],
                   v_hi[:, :, :].bitcast(F32), ALU.subtract).then_inc(v_split, 1)

            def split_probs(u):
                for b in range(2):
                    dve.wait_ge(p_hi_ok, 2 * u + b + 1)
                    tt(p_lo[:, b, :], probs[:, b, 0:SEQ], p_hi[:, b, :].bitcast(F32),
                       ALU.subtract).then_inc(p_split, 1)

            def add_y(u, g, t):
                dve.wait_ge(y_done, 4 * u + t + 1)
                if t == 0:
                    wait(dve, y_added, 4 * u)
                tt(resid[:, 4 * g + t, :], resid[:, 4 * g + t, :], YB[t % 2][:, :], ALU.add).then_inc(y_added, 1)

            def gate(u):
                dve.wait_ge(mixed, u + 1)
                dve.wait_ge(evacuated, PROJ * u + G + 1)
                stt(gated[:, :], g_t[:, :], 1.0, OT[:, :], ALU.add, ALU.mult).then_inc(gate_done, 1)
                wait(dve, y_done, 4 * u)
                dve.wait_ge(gate_done, u + 1)
                v.tensor_copy(u_hi[:, :], gated[:, :]).then_inc(u_hi_ok, 1)
                dve.wait_ge(u_hi_ok, u + 1)
                tt(u_lo[:, :], gated[:, :], u_hi[:, :].bitcast(F32), ALU.subtract).then_inc(u_ok, 1)

            def split_x(g, kt):
                dve.wait_ge(x_hi_ok, KT * g + kt + 1)
                tt(x_lo[:, g, kt, :], resid[:, 4 * g + kt, :], x_hi[:, g, kt, :].bitcast(F32),
                   ALU.subtract).then_inc(x_lo_ok, 1)

            def unit(h, g, lag1=True, lag2=True, split=None, final=False):
                u = GROUPS * h + g
                h1 = h if g >= 1 else h - 1
                if g == 1:
                    dve.wait_ge(decays_ok, h + 1)
                if lag1:
                    mask(h1, u - 1, 0)
                    mask(h1, u - 1, 1)
                    split_v(u - 1)
                if g == 0 and lag1:
                    split_w(h, G)
                if lag2:
                    add_y(u - 2, (g - 2) % GROUPS, 0)
                    add_y(u - 2, (g - 2) % GROUPS, 1)
                if lag1:
                    split_probs(u - 1)
                split_q(u)
                if lag2:
                    add_y(u - 2, (g - 2) % GROUPS, 2)
                    add_y(u - 2, (g - 2) % GROUPS, 3)
                split_k(u)
                if split:
                    for kt in range(KT):
                        split_x(split, kt)
                if final:
                    mean_squares(0, 1)
                    dve.wait_ge(rms_ok, 1)
                    input_sum(0)
                    input_norm(0)
                if lag1:
                    gate(u - 1)

            dve.wait_ge(slopes_in, 16)
            ts(neg_slope[:, :], slope_in[:, :], -1.0, None, ALU.mult).then_inc(dve_const, 1)
            split_w(0, Q)
            for kt in range(KT):
                split_x(0, kt)
            for j in (K, V, G):
                split_w(0, j)
            dve.wait_ge(small_in, 16 * 3)
            split_wo(0)

            for g in range(GROUPS):
                if g >= 2:
                    dve.wait_ge(x_zeroed, g - 1)
                unit(0, g, g >= 1, g >= 2, split=g + 1 if g < GROUPS - 1 else None)
            for j in (Q, K, V):
                split_w(1, j)
            dve.wait_ge(x_zeroed, GROUPS)

            def head(h, after_unit):
                last = isinstance(h, int) and h == HEADS - 1
                for g in range(GROUPS):
                    unit(h, g, final=last and g == GROUPS - 1)
                    if g == 1:
                        split_wo(h)
                    after_unit(g)
                    if g == GROUPS - 1 and not last:
                        for j in (Q, K, V):
                            split_w(h + 1, j)

            with dve.Fori(1, ABS_HEADS + 1) as h:
                def magnitude(g):
                    c = 4 * h - 4 + g
                    dve.wait_ge(fraw_in, 16 * c + 16)
                    v.tensor_reduce(abs_sum[:, bass.ds(c, 1)], w_raw[:, :], axis=AX_X, op=ALU.add,
                                    apply_absolute_value=True).then_inc(abs_ok, 1)

                head(h, magnitude)
            dve.wait_ge(abs_ok, CHUNKS)
            v.tensor_reduce(abs_two[:, :], abs_sum[:, :].rearrange("p (a b) -> p a b", a=2), axis=AX_X,
                            op=ALU.add).then_inc(abs_two_ok, 1)
            dve.wait_ge(gamma_ok, 1)
            half_n = 0.5 / (HID * INNER)
            for k in range(2):
                cols = thr[:, k, :].rearrange("p (a b) -> p a b", a=2)
                src = SC[0][:, 0:2].rearrange("p (a b) -> p a b", b=1).broadcast_to([P, 2, CHUNKS // 2])
                sign = (1.0, -1.0)[k]
                ts(cols, src, sign * half_n, sign * 0.5 * FFN_EPS, ALU.mult, ALU.add).then_inc(thr_ok, 1)
            ts(wscale[:, :], SC[0][:, 0:2], -1.0 / (HID * INNER * Q_B), None, ALU.mult).then_inc(thr_ok, 1)
            dve.wait_ge(thr_ok, 3)

            def ternarise(c):
                cc = bass.ds(c, 1)
                dve.wait_ge(fraw_in, 16 * (CHUNKS + c) + 16)
                ts(tern[:, cc, :], w_raw[:, :], thr[:, 0, cc], None, ALU.is_gt).then_inc(picked, 1)
                dve.wait_ge(picked, c + 1)
                stt(tern[:, cc, :], w_raw[:, :], thr[:, 1, cc], tern[:, cc, :], ALU.is_lt, ALU.subtract).then_inc(terned, 1)

            h0 = ABS_HEADS + 1
            with dve.Fori(h0, h0 + TERN_HEADS) as h:
                head(h, lambda g: ternarise(2 * h - 2 * h0 + g // 2) if g % 2 == 0 else None)
            with dve.Fori(h0 + TERN_HEADS, HEADS - 1) as h:
                head(h, lambda g: None)
            class Count:

                def __init__(self):
                    self.base, self.n = 0, 0

                def next(self):
                    self.n += 1
                    return self.base + self.n

            steps = Count()

            def link(ins):
                ins.then_inc(dstep, 1)
                dve.wait_ge(dstep, steps.next())

            def step(ins):
                ins.then_inc(dstep, 1)
                return steps.next()

            def after(value):
                dve.wait_ge(dstep, value)

            def bn(k, t, src):
                return step(v.bn_stats(stats[:, k, t, :], src))

            def aggregate(k):
                return [step(v.bn_aggr(mv[:, k, t, :], stats[:, k, t, :])) for t in range(BT)]

            def variances(k, eps, aggregated):
                after(aggregated[0])
                step(ts(var_e[:, k, 0:1], mv[:, k, 0, 1:2], eps, None, ALU.add))
                after(aggregated[1])
                ts(var_e[:, k, 1:2], mv[:, k, 1, 1:2], eps, None, ALU.add).then_inc(var_ok[k], 1)

            def norm_stats(k, srcs, eps):
                after(bn(k, 0, srcs[0]))
                bn(k, 1, srcs[1])
                after(step(v.bn_aggr(mv[:, k, 0, :], stats[:, k, 0, :])))
                step(ts(var_e[:, k, 0:1], mv[:, k, 0, 1:2], eps, None, ALU.add))
                after(step(v.bn_aggr(mv[:, k, 1, :], stats[:, k, 1, :])))
                ts(var_e[:, k, 1:2], mv[:, k, 1, 1:2], eps, None, ALU.add).then_inc(var_ok[k], 1)

            def shift(k, b):
                dve.wait_ge(rstd_ok[k], b + 1)
                stt(nshift[:, k, :], mv[:, k, :, 0], -1.0, rstd[:, k, :], ALU.mult, ALU.mult).then_inc(shift_ok[k], 1)

            def normalise(k, b, t, dst, src, done):
                if t == 0:
                    dve.wait_ge(rstd_ok[k], b + 1)
                ts(dst, src, mv[:, k, t, 0:1], rstd[:, k, t:t + 1], ALU.subtract, ALU.mult).then_inc(done, 1)

            def input_sum(b):
                dve.wait_ge(xin_in, 16 * b + 16)
                wait(dve, x1_turned, b)
                for t in range(BT):
                    i = bass.ds(BT * b + t, 1)
                    link(stt(x1[:, t, :], resid[:, i, :], rms[:, i], x_in[:, t, :], ALU.mult, ALU.add))
                norm_stats(NX, [x1[:, t, :] for t in range(BT)], LN_EPS)

            def input_norm(b):
                for t in range(BT):
                    normalise(NX, b, t, x1[:, t, :], x1[:, t, :], x1_ok)

            def maximum(b, c):
                v.tensor_tensor_scan(pp[:, c, 1:SQ], wneg[:, c:c + 1].broadcast_to([P, SEQ]), key[:, c, :],
                                     NEG_BIG, ALU.add, ALU.max).then_inc(pp_ok, 1)

            def maxima(b):
                dve.wait_ge(key_ok, 2 * b + 2)
                for c in range(KT):
                    maximum(b, c)

            def differences(b):
                dve.wait_ge(pp_ok, KT * b + KT)
                tt(t1[:, :, :], pp[:, :, 0:SEQ], pp[:, :, 1:SQ], ALU.subtract).then_inc(t1d_ok, 1)

            def bounded(b):
                dve.wait_ge(kd_ok, 2 * b + 2)
                for c in range(KT):
                    ts(e1[:, c, :], t2[:, c, :], fst[:, c:c + 1], 0.0, ALU.add, ALU.max).then_inc(bounds_ok, 1)
                for c in range(KT):
                    ts(e2[:, c, :], t2[:, c, :], fst[:, c:c + 1], 0.0, ALU.add, ALU.min).then_inc(bounds_ok, 1)

            def bb_states(b):
                dve.wait_ge(e1b_ok, KT * b + KT)
                dve.wait_ge(e2b_ok, b + 1)
                for c in range(KT):
                    v.tensor_tensor_scan(bb[:, c, 1:SQ], e1b[:, c, :], e2b[:, c, :], 0.0,
                                         ALU.mult, ALU.add).then_inc(scans_ok, 1)

            def aa_states(b, counted=None):
                dve.wait_ge(bv_ok, b + 1)
                for c in range(KT):
                    if c == 1 and counted is not None:
                        after(counted)
                    v.tensor_tensor_scan(aa[:, c, 1:SQ], e1b[:, c, :], t1[:, c, :], 0.0,
                                         ALU.mult, ALU.add).then_inc(scans_ok, 1)

            def invert(b):
                dve.wait_ge(den_ok, b)
                v.reciprocal(den[:, :, :], den[:, :, :]).then_inc(inv_ok, 1)

            def quantise_x(b):
                for t in range(BT):
                    ts(xq[:, t, :], xq[:, t, :], qs_x[:, t:t + 1], Q_B, ALU.mult, ALU.min).then_inc(xq_ok, 1)

            def split_x(b):
                for t in range(BT):
                    n = BT * b + t
                    dve.wait_ge(xqh_ok, n + 1)
                    stt(xq_lo[:, t, :, :], QT[t][:, :].rearrange("p (a b) -> p a b", a=KT), -Q_B, xq_hi[:, t, :, :],
                        ALU.max, ALU.subtract).then_inc(xql_ok, 1)

            def split_hidden(b, t):
                for j in range(4):
                    k = 4 * (BT * b + t) + j + 1
                    dve.wait_ge(hqh_ok, k)
                    stt(hq_lo[:, t, 4 * j:4 * j + 4, :], HT[j][:, :].rearrange("p (a b) -> p a b", a=4), -Q_B,
                        hq_hi[:, t, 4 * j:4 * j + 4, :], ALU.max, ALU.subtract).then_inc(hql_ok, 1)

            def first_norms(b, s, b_result, final):
                dve.wait_ge(r_turned, b + 1)
                r0 = bn(NR, 0, TR[0][:, :])
                r1 = bn(NR, 1, TR[1][:, :])
                if final:
                    after(r1)
                else:
                    n = b + 1
                    dve.wait_ge(xin_in, 16 * n + 16)
                    dve.wait_ge(x1_turned, n)
                    i = bass.ds(BT * n, 1)
                    sum0 = step(stt(x1[:, 0, :], resid[:, i, :], rms[:, i], x_in[:, 0, :], ALU.mult, ALU.add))
                    after(r1)
                    i = bass.ds(BT * n + 1, 1)
                    sum1 = step(stt(x1[:, 1, :], resid[:, i, :], rms[:, i], x_in[:, 1, :], ALU.mult, ALU.add))
                variances(NR, LN_EPS, aggregate(NR))
                if not final:
                    after(sum0)
                    bn(NX, 0, x1[:, 0, :])
                    after(sum1)
                    x_last = bn(NX, 1, x1[:, 1, :])
                if not final:
                    after(x_last)
                shift(NR, b)
                if not final:
                    variances(NX, LN_EPS, aggregate(NX))
                for t in range(BT):
                    dve.wait_ge(x2_ok, BT * b + t + 1)
                    q_last = bn(NQ, t, x2[:, s, t, :])
                    if t == 0 and not final:
                        shift(NX, b + 1)
                after(q_last)
                if b_result is not None:
                    dve.wait_ge(rstd_ok[NH], b_result + 1)
                    step(tt(sc_pr[:, :], amax_h[:, :], rstd[:, NH, :], ALU.mult))
                aggregated = aggregate(NQ)
                variances(NQ, FFN_EPS, aggregated)
                centred = [step(ts(xq[:, t, :], x2[:, s, t, :], mv[:, NQ, t, 0:1], None, ALU.subtract))
                           for t in range(BT)]
                for t in range(BT):
                    after(centred[t])
                    largest = step(v.tensor_reduce(amax_x[:, t:t + 1], xq[:, t, :], axis=AX_X, op=ALU.max,
                                                   apply_absolute_value=True))
                if not final:
                    dve.wait_ge(key_ok, 2 * b + 4)
                    maximum(b + 1, 0)
                after(largest)
                inverse = step(v.reciprocal(qs_x[:, :], amax_x[:, :]))
                if not final:
                    maximum(b + 1, 1)
                after(inverse)
                scale = step(ts(qs_x[:, :], qs_x[:, :], Q_B, None, ALU.mult))
                if not final:
                    maximum(b + 1, 2)
                    maximum(b + 1, 3)
                after(scale)
                quantise_x(b)

            def result_sums(b, s):
                for t in range(BT):
                    dve.wait_ge(pr_done, BT * b + t + 1)
                    if t == 0:
                        wait(dve, stored, 16 * b)
                        dve.wait_ge(scpr_ok, b + 1)
                    stt(y_out[:, t, :], PR[t][:, :], sc_pr[:, t:t + 1], x2[:, s, t, :], ALU.mult,
                        ALU.add).then_inc(pr_read, 1)
                for t in range(BT):
                    dve.wait_ge(pr_read, BT * b + t + 1)
                    last = bn(NO, t, y_out[:, t, :])
                return last

            def row(b, s, first=False, final=False):
                first_norms(b, s, None if first else b - 1, final)
                if not final:
                    differences(b + 1)
                dve.wait_ge(rstd_ok[NQ], b + 1)
                part = step(tt(sc_fc[:, :], amax_x[:, :], rstd[:, NQ, :], ALU.mult))
                split_x(b)
                after(part)
                ts(sc_fc[:, :], sc_fc[:, :], wscale[:, 0:1], None, ALU.mult).then_inc(scfc_ok, 1)
                if not final:
                    bounded(b + 1)
                if not final:
                    bb_states(b + 1)
                    dve.wait_ge(ctx_in, 16 * b + 32)
                    tt(t1[:, :, :], e2b[:, :, :], val[:, :, :], ALU.mult).then_inc(bv_ok, 1)
                if not first:
                    ts(sc_pr[:, :], sc_pr[:, :], wscale[:, 1:2], None, ALU.mult).then_inc(scpr_ok, 1)
                    y_last = result_sums(b - 1, 1 - s)
                if not final:
                    aa_states(b + 1, y_last if not first else None)
                elif not first:
                    after(y_last)
                if not first:
                    variances(NO, LN_EPS, aggregate(NO))
                if not final:
                    invert(b + 1)
                for t in range(BT):
                    n = BT * b + t
                    dve.wait_ge(cent_ok, n + 1)
                    a, q = amax_h[:, t:t + 1], qs_h[:, t:t + 1]
                    largest = step(v.tensor_reduce(a, hid[:, t, :], axis=AX_X, op=ALU.max,
                                                   apply_absolute_value=True))
                    if t == 1 and not first:
                        shift(NO, b - 1)
                    after(largest)
                    inverse = step(v.reciprocal(q, a))
                    after(inverse)
                    scale = step(ts(q, q, Q_B, None, ALU.mult))
                    dve.wait_ge(hsq_ok, n + 1)
                    after(scale)
                    ts(hid[:, t, :], hid[:, t, :], q, Q_B, ALU.mult, ALU.min).then_inc(hq_ok, 1)
                    if final and t == 0:
                        split_hidden(b, 0)
                ts(var_e[:, NH, :], hssq[:, :], 1.0 / INNER, FFN_EPS, ALU.mult, ALU.add).then_inc(var_ok[NH], 1)
                for t in range(1 if final else 0, BT):
                    split_hidden(b, t)

            def mean_squares(g0, g1):
                n = 1 if g0 == 0 else 2
                dve.wait_ge(sq_total, n)
                c = slice(KT * g0, KT * g1)
                ts(rms_in[:, c], VT[:, c], 1.0 / INNER, RMS_EPS, ALU.mult, ALU.add).then_inc(rms_in_ok, 1)

            def first_fraction():
                dve.wait_ge(e1_ok, 1)
                dve.wait_ge(e2_ok, 1)
                dve.wait_ge(scans_ok, 2 * KT)
                link(tt(den[:, :, :], e1[:, :, :], bb[:, :, 0:SEQ], ALU.mult))
                link(tt(den[:, :, :], den[:, :, :], e2[:, :, :], ALU.add))
                for t in range(2):
                    add_y(UNITS - 1, (UNITS - 1) % GROUPS, t)
                link(v.reciprocal(den[:, :, :], den[:, :, :]))
                dve.wait_ge(num_ok, 1)
                link(tt(num[:, :, :], num[:, :, :], den[:, :, :], ALU.mult))
                tt(num[:, :, :], num[:, :, :], key[:, :, :], ALU.add).then_inc(r_ok, 1)

            dve.wait_ge(wneg_exp, 1)
            ts(wneg[:, :], wneg[:, :], -1.0, None, ALU.mult).then_inc(w_ok, 1)
            dve.wait_ge(w_ok, 1)
            head(HEADS - 1, lambda g: None)
            U = UNITS
            mask(HEADS - 1, U - 1, 0)
            mask(HEADS - 1, U - 1, 1)
            split_v(U - 1)
            split_probs(U - 1)
            dve.wait_ge(states0, 3)
            maxima(0)
            for t in range(2):
                add_y(U - 2, (U - 2) % GROUPS, t)
            differences(0)
            for c in (0, 2):
                tt(t2[:, c:c + 2, :], key[:, c:c + 2, :], pp[:, c:c + 2, 0:SEQ], ALU.subtract).then_inc(kd_ok, 1)
            bounded(0)
            for t in range(2, 4):
                add_y(U - 2, (U - 2) % GROUPS, t)
            bb_states(0)
            aa_states(0)
            gate(U - 1)
            first_fraction()
            for t in range(2, 4):
                add_y(U - 1, (U - 1) % GROUPS, t)
            mean_squares(1, GROUPS)
            s0 = steps.n
            row(0, 0, first=True)
            dve.wait_ge(rms_ok, 2)
            dve.wait_ge(y_added, 4 * UNITS)
            s1 = steps.n
            row_steps = s1 - s0 + 6
            with dve.Fori(0, (BATCH - 2) // 2) as i:
                steps.base, steps.n = 2 * row_steps * i + s1, 0
                row(2 * i + 1, 1)
                assert steps.n == row_steps
                row(2 * i + 2, 0)
                assert steps.n == 2 * row_steps
            steps.base, steps.n = (BATCH - 2) * row_steps + s1, 0
            row(BATCH - 1, (BATCH - 1) % 2, final=True)
            b, s = BATCH - 1, (BATCH - 1) % 2
            dve.wait_ge(rstd_ok[NH], b + 1)
            link(tt(sc_pr[:, :], amax_h[:, :], rstd[:, NH, :], ALU.mult))
            ts(sc_pr[:, :], sc_pr[:, :], wscale[:, 1:2], None, ALU.mult).then_inc(scpr_ok, 1)
            after(result_sums(b, s))
            variances(NO, LN_EPS, aggregate(NO))
            shift(NO, b)

        @block.gpsimd
        def _(pool):
            g_ = nc.gpsimd
            g_.memset(ident[:, :], 0.0).then_inc(pool_const, 1)
            g_.memset(ones[:, :], 1.0).then_inc(pool_const, 1)
            g_.memset(neg_half[:, :], -0.5).then_inc(pool_const, 1)
            g_.memset(sq_sum[:, :, :], 0.0).then_inc(pool_const, 1)
            g_.iota(dist_i, [[1, SEQ]], 0, -1).then_inc(dist_ok, 1)
            pool.wait_ge(dist_ok, 1)
            g_.tensor_scalar(dist[:, :], dist_i, 0.0, None, ALU.max).then_inc(dist_ok, 1)
            pool.wait_ge(pool_const, 4)
            g_.affine_select(out=ident[:, :], in_=ident[:, :], compare_op=ALU.not_equal, fill=1.0, base=0,
                             pattern=[[-1, P]], channel_multiplier=1).then_inc(ident_ok, 1)
            g_.affine_select(out=tri[:, :], in_=ones[:, :], compare_op=ALU.is_ge, fill=0.0, base=0,
                             pattern=[[1, P]], channel_multiplier=-1).then_inc(tri_ok, 1)
            pool.wait_ge(tri_ok, 1)

            def cut_decay(h):
                pool.wait_ge(decay_exp, h + 1)
                d = decays[:, bass.ds(h & 1, 1), 0:P]
                g_.tensor_tensor(d, d, tri[:, :], ALU.mult).then_inc(decays_ok, 1)

            def clear(g):
                pool.wait_ge(x_lo_ok, KT * (g + 1))
                g_.memset(resid[:, 4 * g:4 * g + 4, :], 0.0).then_inc(x_zeroed, 1)

            def add_squares(u, g):
                pool.wait_ge(squared, u + 1)
                wait(pool, sq_added, u - GROUPS + 1)
                g_.tensor_tensor(sq_sum[:, g, :], sq_sum[:, g, :], o_sq[:, :], ALU.add).then_inc(sq_added, 1)

            cut_decay(0)
            for g in range(GROUPS):
                clear(g)
                if g >= 1:
                    add_squares(g - 1, g - 1)
                if g == 1:
                    cut_decay(1)
            add_squares(GROUPS - 1, GROUPS - 1)
            with pool.Fori(1, HEADS - 1) as h:
                for g in range(GROUPS):
                    add_squares(GROUPS * h + g, g)
                    if g == 0:
                        cut_decay(h + 1)
            for g in range(GROUPS - 2):
                add_squares(GROUPS * (HEADS - 1) + g, g)

            def rms_root(g0, g1):
                pool.wait_ge(rms_in_ok, 1 if g0 == 0 else 2)
                c = slice(KT * g0, KT * g1)
                g_.tensor_tensor(rms[:, c], rms_in[:, c], neg_half[:, c], ALU.pow).then_inc(rms_ok, 1)

            rms_root(0, 1)
            def root(k, b):
                pool.wait_ge(var_ok[k], b + 1)
                g_.tensor_tensor(rstd[:, k, :], var_e[:, k, :], neg_half[:, 0:BT], ALU.pow).then_inc(rstd_ok[k], 1)

            def numerator(b):
                pool.wait_ge(pp_ok, KT * b + KT)
                g_.tensor_tensor(e2b[:, :, :], key[:, :, :], pp[:, :, 1:SQ], ALU.subtract).then_inc(e2d_ok, 1)
                pool.wait_ge(ctx_in, 16 * b + 16)
                pool.wait_ge(e2b_ok, b + 1)
                pool.wait_ge(e1b_ok, KT * b + KT)
                g_.tensor_tensor(t1[:, :, :], e2b[:, :, :], val[:, :, :], ALU.mult).then_inc(bv_ok, 1)
                pool.wait_ge(e2_ok, b + 1)
                g_.tensor_tensor(t2[:, :, :], e2[:, :, :], val[:, :, :], ALU.mult).then_inc(ev_ok, 1)
                pool.wait_ge(e1_ok, b + 1)
                pool.wait_ge(scans_ok, 2 * KT * (b + 1))
                g_.tensor_tensor(num[:, :, :], e1[:, :, :], aa[:, :, 0:SEQ], ALU.mult).then_inc(num1_ok, 1)
                pool.wait_ge(num1_ok, b + 1)
                pool.wait_ge(ev_ok, b + 1)
                g_.tensor_tensor(num[:, :, :], num[:, :, :], t2[:, :, :], ALU.add).then_inc(num_ok, 1)

            def wkv(b):
                for c in (0, 2):
                    pool.wait_ge(pp_ok, KT * b + c + 2)
                    g_.tensor_tensor(t2[:, c:c + 2, :], key[:, c:c + 2, :], pp[:, c:c + 2, 0:SEQ],
                                     ALU.subtract).then_inc(kd_ok, 1)
                g_.tensor_tensor(e2b[:, :, :], key[:, :, :], pp[:, :, 1:SQ], ALU.subtract).then_inc(e2d_ok, 1)
                pool.wait_ge(e1_ok, b + 1)
                pool.wait_ge(scans_ok, 2 * KT * b + KT)
                g_.tensor_tensor(den[:, :, :], e1[:, :, :], bb[:, :, 0:SEQ], ALU.mult).then_inc(den1_ok, 1)
                pool.wait_ge(e2_ok, b + 1)
                pool.wait_ge(den1_ok, b)
                g_.tensor_tensor(den[:, :, :], den[:, :, :], e2[:, :, :], ALU.add).then_inc(den_ok, 1)
                wait(pool, r_turned, b)
                pool.wait_ge(scans_ok, 2 * KT * (b + 1))
                g_.tensor_tensor(num[:, :, :], e1[:, :, :], aa[:, :, 0:SEQ], ALU.mult).then_inc(num1_ok, 1)
                pool.wait_ge(ctx_in, 16 * b + 16)
                g_.tensor_tensor(t2[:, :, :], e2[:, :, :], val[:, :, :], ALU.mult).then_inc(ev_ok, 1)
                pool.wait_ge(num1_ok, b + 1)
                pool.wait_ge(ev_ok, b + 1)
                g_.tensor_tensor(num[:, :, :], num[:, :, :], t2[:, :, :], ALU.add).then_inc(num_ok, 1)
                pool.wait_ge(inv_ok, b)
                pool.wait_ge(num_ok, b + 1)
                g_.tensor_tensor(num[:, :, :], num[:, :, :], den[:, :, :], ALU.mult).then_inc(y_ok, 1)
                pool.wait_ge(y_ok, b)
                g_.tensor_tensor(num[:, :, :], num[:, :, :], key[:, :, :], ALU.add).then_inc(r_ok, 1)

            def row(b, first=False, final=False):
                root(NR, b)
                if not final:
                    root(NX, b + 1)
                root(NQ, b)
                if not final:
                    wkv(b + 1)
                if not first:
                    root(NO, b - 1)
                root(NH, b)

            root(NX, 0)
            add_squares(UNITS - 2, GROUPS - 2)
            pool.wait_ge(projected, PROJ * UNITS)
            g_.memset(pp[:, :, 0:1], NEG_BIG).then_inc(states0, 1)
            g_.memset(aa[:, :, 0:1], 0.0).then_inc(states0, 1)
            g_.memset(bb[:, :, 0:1], 0.0).then_inc(states0, 1)
            numerator(0)
            add_squares(UNITS - 1, GROUPS - 1)
            rms_root(1, GROUPS)
            row(0, first=True)
            with pool.Fori(1, BATCH - 1) as b:
                row(b)
            row(BATCH - 1, final=True)
            root(NO, BATCH - 1)


def kernel(x, ctx_2048, L0_attn_slope_rate, L0_attn_Wqkv, L0_attn_Wg, L0_attn_norm_w, L0_attn_Wo,
           L0_xattn_time_decay, L0_xattn_time_first, L0_ffn_w_fc, L0_ffn_w_proj):
    import numpy as np
    import concourse.bacc as bacc
    from concourse.bass_utils import run_bass_kernel_spmd

    def tiled(w_t):
        return w_t.reshape(-1, P, w_t.shape[1]).transpose(1, 0, 2)

    x = np.asarray(x)
    x_t = tiled(x.reshape(TOKENS, HID).T).reshape(P, KT, GROUPS, GT).transpose(0, 2, 1, 3)
    x_rows = x.reshape(BATCH, BT, P, HID).transpose(0, 2, 1, 3)
    ctx_t = np.asarray(ctx_2048).reshape(BATCH, SEQ, KT, P).transpose(0, 3, 2, 1)
    qkv = np.asarray(L0_attn_Wqkv).reshape(HEADS, 3, DH, KT, P).transpose(0, 4, 1, 3, 2)
    gate = np.asarray(L0_attn_Wg).reshape(HEADS, 1, DH, KT, P).transpose(0, 4, 1, 3, 2)
    wo = np.asarray(L0_attn_Wo).T.reshape(HEADS, P, 1, HID)
    w_heads = np.concatenate([qkv.reshape(HEADS, P, 3, HID), gate.reshape(HEADS, P, 1, HID), wo], axis=2)
    slopes = np.broadcast_to(np.asarray(L0_attn_slope_rate).reshape(1, HEADS), (P, HEADS))
    norm_w = np.asarray(L0_attn_norm_w).reshape(HEADS, P).T
    decay = np.asarray(L0_xattn_time_decay).reshape(KT, P).T
    first = np.asarray(L0_xattn_time_first).reshape(KT, P).T
    w_ffn = np.concatenate([tiled(np.asarray(L0_ffn_w_fc).T).reshape(P, -1),
                            tiled(np.asarray(L0_ffn_w_proj).T).reshape(P, -1)], axis=1)
    w_ffn = w_ffn.reshape(P, CHUNKS, CW).transpose(1, 0, 2)
    laid = {"x_t": x_t, "x_rows": x_rows, "ctx_t": ctx_t, "w_heads": w_heads, "slopes": slopes,
            "norm_w": norm_w, "decay": decay, "first": first, "w_ffn": w_ffn}
    laid = {k: np.ascontiguousarray(a) for k, a in laid.items()}

    nc = bacc.Bacc("TRN2", target_bir_lowering=False, num_devices=1)
    args = {k: nc.dram_tensor(k, a.shape, F32, kind="ExternalInput").ap() for k, a in laid.items()}
    out = nc.dram_tensor("out", (BATCH, P, BT, HID), F32, kind="ExternalOutput").ap()
    decoder_layer(nc, **args, out=out)
    r = run_bass_kernel_spmd(nc, [laid], core_ids=[0])
    got = np.asarray(r.results[0]["out"])
    return got.transpose(0, 2, 1, 3).reshape(BATCH, SEQ, HID)
```
